# Optimizing a Trainium2 kernel written in Bass

```python
import numpy as np
import jax
import jax.numpy as jnp

def _softmax(x, axis=-1):
    return jax.nn.softmax(x, axis=axis)

def _gelu(x):
    return jax.nn.gelu(x, approximate=True)

def _silu(x):
    return jax.nn.silu(x)

def _sigmoid(x):
    return jax.nn.sigmoid(x)

def _layernorm(x, axis=-1, eps=1e-05):
    m = jnp.mean(x, axis=axis, keepdims=True)
    v = jnp.var(x, axis=axis, keepdims=True)
    return (x - m) / jnp.sqrt(v + eps)

def _scatter_add(tgt, idx, src, axis=0):
    return tgt.at[idx].add(src)

def _segment_sum(src, seg, n):
    return jax.ops.segment_sum(src, seg, n)
kernel_name = 'mk_flamingo_gated_d4_seqx_r8_59416d'

def setup_inputs(seed: int=0):
    np.random.seed(seed)
    _w = jnp.asarray

    def _rec_inputs():
        import jax
        import jax.numpy as jnp
        _rk = jax.random.key(seed)
        x = 2.818e-05 + 1 * jax.random.normal(jax.random.fold_in(_rk, 1), (64, 64, 128), jnp.float32)
        _lenS = 64 - jax.random.randint(jax.random.fold_in(_rk, 7), (64,), 0, max(1, 64 // 4) + 1, jnp.int32)
        _lenS2 = 64 - jax.random.randint(jax.random.fold_in(_rk, 8), (64,), 0, max(1, 64 // 4) + 1, jnp.int32)
        _ctx_2048P = jax.random.normal(jax.random.fold_in(_rk, 11), (64, 16, 256), jnp.float32)
        _ctx_2048c = jax.random.dirichlet(jax.random.fold_in(_rk, 511), 0.3 * jnp.ones((16,), jnp.float32), (64, 64))
        _ctx_2048t = jnp.einsum('bsk,bkd->bsd', _ctx_2048c, _ctx_2048P)
        _ctx_2048t = _ctx_2048t * jax.lax.rsqrt(jnp.mean(jnp.square(_ctx_2048t)) + 1e-12) * 0.953939
        ctx_2048 = -0.000125008 + 0.999885 * (_ctx_2048t + 0.3 * jax.random.normal(jax.random.fold_in(_rk, 611), (64, 64, 256), jnp.float32))
        _validS = jnp.arange(64)[None, :] < _lenS[:, None]
        _validS2 = jnp.arange(64)[None, :] < _lenS2[:, None]
        _causal = jnp.tril(jnp.ones((64, 64), dtype=bool))
        mask_BxS2_fk1 = jnp.where(jnp.broadcast_to(_validS2[:, :], (64, 64)), 1.0, 0.0).astype(jnp.float32)
        mask_BxS2_if0 = jnp.where(jnp.ones((64, 64), dtype=bool), 4, 0).astype(jnp.int32)
        mask_BxS2_ik0 = jnp.where(jnp.broadcast_to(_validS2[:, :], (64, 64)), 0, 1).astype(jnp.int32)
        _g = jax.random.normal(jax.random.fold_in(_rk, 9001), (2, 4), jnp.float32)
        _g = jnp.sign(_g) * jnp.maximum(jnp.abs(_g), 1.0) + (_g == 0) * 1.0
        g_xattn = _g[0]
        g_ffn = _g[1]
        return (x, ctx_2048, mask_BxS2_fk1, mask_BxS2_if0, mask_BxS2_ik0, g_xattn, g_ffn)
    x, ctx_2048, mask_BxS2_fk1, mask_BxS2_if0, mask_BxS2_ik0, g_xattn, g_ffn = _rec_inputs()

    def _L0_xattn_setup():
        import jax, jax.numpy as jnp
        import numpy as np
        B, S, T = (32, 64, 64)
        SRC_SIZE, TGT_SIZE, OUT_SIZE, NUM_HEAD = (256, 128, 128, 8)
        HEAD_DIM = OUT_SIZE // NUM_HEAD
        key = jax.random.key(seed)
        ks = jax.random.split(key, 12)
        src = jax.random.normal(ks[0], (B, S, SRC_SIZE), dtype=jnp.float32)
        tgt = jax.random.normal(ks[1], (B, T, TGT_SIZE), dtype=jnp.float32)
        src_mask = (jax.random.uniform(ks[2], (B, S)) > 0.3).astype(jnp.float32)
        src_mask = src_mask.at[:, 0].set(1.0)
        tgt_mask = (jax.random.uniform(ks[3], (B, T)) > 0.3).astype(jnp.float32)
        tgt_mask = tgt_mask.at[:, 0].set(1.0)

        def lin(k, out_f, in_f):
            return jax.random.normal(k, (out_f, in_f), dtype=jnp.float32) / np.sqrt(in_f)
        W_src = lin(ks[4], 2 * OUT_SIZE, SRC_SIZE)
        b_src = jnp.zeros((2 * OUT_SIZE,), jnp.float32)
        W_tgt = lin(ks[5], OUT_SIZE, TGT_SIZE)
        b_tgt = jnp.zeros((OUT_SIZE,), jnp.float32)
        W_out = lin(ks[6], OUT_SIZE, OUT_SIZE + TGT_SIZE)
        b_out = jnp.zeros((OUT_SIZE,), jnp.float32)
        return {'src': src, 'tgt': tgt, 'src_mask': src_mask, 'tgt_mask': tgt_mask, 'W_src': W_src, 'b_src': b_src, 'W_tgt': W_tgt, 'b_tgt': b_tgt, 'W_out': W_out, 'b_out': b_out}
    _L0_xattn_all = _L0_xattn_setup()
    _L0_xattn_in = {k: v for k, v in _L0_xattn_all.items() if k in ('W_src', 'b_src', 'W_tgt', 'b_tgt', 'W_out', 'b_out')}
    del _L0_xattn_all

    def _L0_ffn_setup():
        import jax, jax.numpy as jnp
        import numpy as np
        DIM = 128
        DEPTH = 2
        HEADS = 8
        DIM_HEAD = 64
        WINDOW = 64
        INNER = HEADS * DIM_HEAD
        HID = int(DIM * 4 * 2 / 3)
        B, N = (2, 1024)
        QK_SCALE = 8.0

        def shift_token(t):
            t1, t2 = jnp.split(t, 2, axis=-1)
            t2 = jnp.pad(t2, ((0, 0), (1, 0), (0, 0)))[:, :-1]
            return jnp.concatenate([t1, t2], axis=-1)

        def l2norm(t):
            return t / jnp.clip(jnp.linalg.norm(t, axis=-1, keepdims=True), 1e-12)

        def rotate_half(x):
            x1, x2 = jnp.split(x, 2, axis=-1)
            return jnp.concatenate([-x2, x1], axis=-1)

        def rotary_xpos(q, k):
            n = q.shape[-2]
            half_idx = jnp.arange(0, DIM_HEAD, 2, dtype=jnp.float32)
            inv_freq = 1.0 / 10000.0 ** (half_idx / DIM_HEAD)
            t = jnp.arange(n, dtype=jnp.float32)
            freqs = t[:, None] * inv_freq[None, :]
            freqs = jnp.concatenate([freqs, freqs], axis=-1)
            base = (half_idx + 0.4 * DIM_HEAD) / (1.4 * DIM_HEAD)
            power = (t - n // 2) / float(WINDOW // 2)
            scale = base[None, :] ** power[:, None]
            scale = jnp.concatenate([scale, scale], axis=-1)
            cos, sin = (jnp.cos(freqs), jnp.sin(freqs))
            q = q * cos * scale + rotate_half(q) * sin * scale
            k = k * cos / scale + rotate_half(k) * sin / scale
            return (q, k)

        def local_attention(q, k, v):
            b, h, n, d = q.shape
            w = n // WINDOW
            bq = q.reshape(b, h, w, WINDOW, d) * QK_SCALE
            bk = k.reshape(b, h, w, WINDOW, d)
            bv = v.reshape(b, h, w, WINDOW, d)

            def look_around(t):
                p = jnp.pad(t, ((0, 0), (0, 0), (1, 0), (0, 0), (0, 0)))
                return jnp.concatenate([p[:, :, :w], p[:, :, 1:]], axis=3)
            bk, bv = (look_around(bk), look_around(bv))
            bt = jnp.arange(n).reshape(w, WINDOW)
            btp = jnp.pad(bt, ((1, 0), (0, 0)), constant_values=-1)
            btk = jnp.concatenate([btp[:w], btp[1:]], axis=1)
            sim = jnp.einsum('bhwid,bhwjd->bhwij', bq, bk)
            i = bt[:, :, None]
            j = btk[:, None, :]
            mask = (i < j) | (i > j + WINDOW) | (j == -1)
            sim = jnp.where(mask, -jnp.finfo(sim.dtype).max, sim)
            attn = jax.nn.softmax(sim, axis=-1)
            out = jnp.einsum('bhwij,bhwjd->bhwid', attn, bv)
            return out.reshape(b, h, n, d)

        def _layer(x, wqkv, qs, ksc, wo, lg, lb, w1, b1, w2, b2):
            b, n, _ = x.shape
            h = shift_token(x)
            qkv = h @ wqkv
            q, k, v = jnp.split(qkv, 3, axis=-1)
            to_heads = lambda t: t.reshape(b, n, HEADS, DIM_HEAD).transpose(0, 2, 1, 3)
            q, k, v = (to_heads(q), to_heads(k), to_heads(v))
            q = l2norm(q) * qs
            k = l2norm(k) * ksc
            q, k = rotary_xpos(q, k)
            o = local_attention(q, k, v)
            o = o.transpose(0, 2, 1, 3).reshape(b, n, INNER)
            x = x + o @ wo
            h = shift_token(x)
            mu = h.mean(-1, keepdims=True)
            var = h.var(-1, keepdims=True)
            h = (h - mu) / jnp.sqrt(var + 1e-05) * lg + lb
            h = h @ w1 + b1
            a, g = jnp.split(h, 2, axis=-1)
            h = a * jax.nn.gelu(g, approximate=False)
            x = x + h @ w2 + b2
            return x
        key = jax.random.key(seed)
        ks = jax.random.split(key, 6)
        return {'x': jax.random.normal(ks[0], (B, N, DIM), jnp.float32), 'wqkv': jax.random.normal(ks[1], (DEPTH, DIM, 3 * INNER), jnp.float32) * 0.02, 'q_scale': jnp.ones((DEPTH, DIM_HEAD), jnp.float32), 'k_scale': jnp.ones((DEPTH, DIM_HEAD), jnp.float32), 'wo': jax.random.normal(ks[2], (DEPTH, INNER, DIM), jnp.float32) * 0.02, 'ln_g': jnp.ones((DEPTH, DIM), jnp.float32), 'ln_b': jnp.zeros((DEPTH, DIM), jnp.float32), 'w1': jax.random.normal(ks[3], (DEPTH, DIM, 2 * HID), jnp.float32) * 0.02, 'b1': jnp.zeros((DEPTH, 2 * HID), jnp.float32), 'w2': jax.random.normal(ks[4], (DEPTH, HID, DIM), jnp.float32) * 0.02, 'b2': jnp.zeros((DEPTH, DIM), jnp.float32)}
    _L0_ffn_all = _L0_ffn_setup()
    _L0_ffn_in = {k: v for k, v in _L0_ffn_all.items() if k in ('wqkv', 'q_scale', 'k_scale', 'wo', 'ln_g', 'ln_b', 'w1', 'b1', 'w2', 'b2')}
    del _L0_ffn_all

    def _L1_xattn_setup():
        import jax, jax.numpy as jnp
        import numpy as np
        B, L, P = (4, 512, 128)
        D_MODEL = 128
        D_GLOBAL = 256
        HEADDIM = 32
        EPSILON = 0.001
        RMS_EPS = 1e-05

        def rmsnorm(x, g, eps=RMS_EPS):
            var = jnp.mean(jnp.square(x), axis=-1, keepdims=True)
            return x * jax.lax.rsqrt(var + eps) * g

        def _hnet_depool(h, h_patch_full, patch_lens):
            h_patch = h_patch_full[..., :D_MODEL]
            bsz, plen = (h_patch.shape[0], h_patch.shape[1])
            seqlen = h.shape[1]
            logp = jnp.full((bsz, plen), -EPSILON, dtype=jnp.float32)
            bidx = jnp.cumsum(patch_lens, axis=1) - 1
            boundary_mask = jnp.zeros((bsz, seqlen), dtype=jnp.int32)
            boundary_mask = boundary_mask.at[jnp.arange(bsz)[:, None], bidx].set(1)
            dt = (-jnp.log(-jnp.expm1(logp))).astype(h_patch.dtype)
            x = h_patch / dt[..., None]
            n_heads = D_MODEL // HEADDIM
            A = -jnp.ones((n_heads,), dtype=jnp.float32)
            bcoef = jnp.exp(logp).astype(h_patch.dtype)
            x4 = x.reshape(bsz, plen, n_heads, HEADDIM)
            a = jnp.exp(dt[:, :, None] * A[None, None, :])
            u = (dt * bcoef)[:, :, None, None] * x4
            a_b = jnp.broadcast_to(a[..., None], u.shape)

            def comb(lft, rgt):
                aL, uL = lft
                aR, uR = rgt
                return (aL * aR, uL * aR + uR)
            _, s = jax.lax.associative_scan(comb, (a_b, u), axis=1)
            depool = s.reshape(bsz, plen, D_MODEL)
            plug = jnp.clip(jnp.cumsum(boundary_mask, axis=1) - 1, 0, plen - 1)
            depool_out = depool[jnp.arange(bsz)[:, None], plug]
            return depool_out + h
        key = jax.random.key(seed)
        k1, k2, k3, k4 = jax.random.split(key, 4)
        embeds = jax.random.normal(k1, (B, L, D_MODEL), dtype=jnp.float32)
        patch_embeds = jax.random.normal(k2, (B, P, D_GLOBAL), dtype=jnp.float32)
        patch_lens = jnp.full((B, P), L // P, dtype=jnp.int64)
        W_in = jax.random.normal(k3, (D_MODEL, D_MODEL), dtype=jnp.float32) * 0.02
        b_in = jnp.zeros((D_MODEL,), dtype=jnp.float32)
        g_res = jnp.ones((D_MODEL,), dtype=jnp.float32)
        g_init = jnp.ones((D_GLOBAL,), dtype=jnp.float32)
        return {'embeds': embeds, 'patch_embeds': patch_embeds, 'patch_lens': patch_lens, 'W_in': W_in, 'b_in': b_in, 'g_res': g_res, 'g_init': g_init}
    _L1_xattn_all = _L1_xattn_setup()
    _L1_xattn_in = {k: v for k, v in _L1_xattn_all.items() if k in ('W_in', 'b_in', 'g_res', 'g_init')}
    del _L1_xattn_all

    def _L1_ffn_setup():
        import jax, jax.numpy as jnp
        import numpy as np
        TOP_K = 2
        key = jax.random.key(seed)
        k1, k2, k3, k4 = jax.random.split(key, 4)
        B_, S, D = (4, 1024, 128)
        E, R = (8, 16)
        x = jax.random.normal(k1, (B_, S, D), dtype=jnp.float32)
        Wg = jax.random.normal(k2, (D, E), dtype=jnp.float32) * 0.02
        A = jax.random.normal(k3, (E, D, R), dtype=jnp.float32) * 0.02
        Bm = jax.random.normal(k4, (E, R, D), dtype=jnp.float32) * 0.02
        return {'x': x, 'Wg': Wg, 'A': A, 'B': Bm}
    _L1_ffn_all = _L1_ffn_setup()
    _L1_ffn_in = {k: v for k, v in _L1_ffn_all.items() if k in ('Wg', 'A', 'B')}
    del _L1_ffn_all

    def _L2_xattn_setup():
        import jax, jax.numpy as jnp
        import numpy as np
        UNITS = 128
        NUM_HEADS = 8

        def _split_heads(x, n):
            B, S, D = x.shape
            return x.reshape(B, S, n, D // n).transpose(0, 2, 1, 3)
        key = jax.random.key(seed)
        k1, k2, k3 = jax.random.split(key, 3)
        B, S = (8, 128)
        memory = jax.random.normal(k1, (B, S, 2 * UNITS), dtype=jnp.float32)
        query = jax.random.normal(k2, (B, S, UNITS), dtype=jnp.float32)
        seq_mask = jax.random.randint(k3, (B, S), 0, 2, dtype=jnp.int32)
        b = jnp.zeros((1,), dtype=jnp.float32)
        return {'memory': memory, 'query': query, 'seq_mask': seq_mask, 'b': b}
    _L2_xattn_all = _L2_xattn_setup()
    _L2_xattn_in = {k: v for k, v in _L2_xattn_all.items() if k in ('b',)}
    del _L2_xattn_all

    def _L2_ffn_setup():
        import jax, jax.numpy as jnp
        import numpy as np
        QB = 127.0
        EPS = 1e-05

        def _ste(x, q):
            return x + jax.lax.stop_gradient(q - x)

        def bitlinear(x, W, b):
            w_scale = jnp.clip(jnp.mean(jnp.abs(W)), EPS, None)
            Wq = _ste(W, jnp.clip(jnp.round(W / w_scale), -1.0, 1.0) * w_scale)
            x_scale = jnp.clip(jnp.max(jnp.abs(x), axis=-1, keepdims=True), EPS, None)
            xq = _ste(x, jnp.clip(jnp.round(x * (QB / x_scale)), -QB - 1.0, QB) * (x_scale / QB))
            return jnp.einsum('bnd,hd->bnh', xq, Wq) + b
        key = jax.random.key(seed)
        k0, k1, k2 = jax.random.split(key, 3)
        B, N, D = (8, 512, 128)
        H = int(D * 4.0)
        x = jax.random.normal(k0, (B, N, D), dtype=jnp.float32)
        W1 = jax.random.normal(k1, (H, D), dtype=jnp.float32) * 0.02
        b1 = jnp.zeros((H,), dtype=jnp.float32)
        W2 = jax.random.normal(k2, (D, H), dtype=jnp.float32) * 0.02
        b2 = jnp.zeros((D,), dtype=jnp.float32)
        return {'x': x, 'W1': W1, 'b1': b1, 'W2': W2, 'b2': b2}
    _L2_ffn_all = _L2_ffn_setup()
    _L2_ffn_in = {k: v for k, v in _L2_ffn_all.items() if k in ('W1', 'b1', 'W2', 'b2')}
    del _L2_ffn_all

    def _L3_xattn_setup():
        import jax, jax.numpy as jnp
        import numpy as np
        NUM_HEADS = 16
        key = jax.random.key(seed)
        ks = jax.random.split(key, 5)
        dim = 128
        B, N, N_c = (4, 128, 32)
        x = jax.random.normal(ks[0], (B, N, dim), dtype=jnp.float32)
        context = jax.random.normal(ks[1], (B, N_c, 2 * dim), dtype=jnp.float32)
        w_qkv = jax.random.normal(ks[2], (3 * dim, dim), dtype=jnp.float32) * 0.02
        w_proj = jax.random.normal(ks[3], (dim, dim), dtype=jnp.float32) * 0.02
        b_proj = jax.random.normal(ks[4], (dim,), dtype=jnp.float32) * 0.02
        return {'x': x, 'context': context, 'w_qkv': w_qkv, 'w_proj': w_proj, 'b_proj': b_proj}
    _L3_xattn_all = _L3_xattn_setup()
    _L3_xattn_in = {k: v for k, v in _L3_xattn_all.items() if k in ('w_qkv', 'w_proj', 'b_proj')}
    del _L3_xattn_all

    def _L3_ffn_setup():
        import jax, jax.numpy as jnp
        import numpy as np
        B, S, D_MODEL, D_HIDDEN = (4, 256, 128, 512)

        def act_quant(x):
            scale = 127.0 / jnp.clip(jnp.max(jnp.abs(x), axis=-1, keepdims=True), 1e-05)
            return jnp.clip(jnp.round(x * scale), -128, 127) / scale

        def weight_quant(w):
            scale = 1.0 / jnp.clip(jnp.mean(jnp.abs(w)), 1e-05)
            return jnp.clip(jnp.round(w * scale), -1, 1) / scale

        def bit_linear(x, w):
            xq = x + jax.lax.stop_gradient(act_quant(x) - x)
            wq = w + jax.lax.stop_gradient(weight_quant(w) - w)
            return jnp.einsum('bsd,hd->bsh', xq, wq)

        def depthwise_conv1d(x_bcl, w, b):
            y = jax.lax.conv_general_dilated(x_bcl, w, window_strides=(1,), padding=[(1, 1)], dimension_numbers=('NCH', 'OIH', 'NCH'), feature_group_count=x_bcl.shape[1])
            return y + b[None, :, None]
        key = jax.random.key(seed)
        ks = jax.random.split(key, 5)
        lim1 = 1.0 / np.sqrt(D_MODEL)
        lim2 = 1.0 / np.sqrt(D_HIDDEN)
        limc = 1.0 / np.sqrt(3.0)
        return {'x': jax.random.normal(ks[0], (B, S, D_MODEL), dtype=jnp.float32), 'w1': jax.random.uniform(ks[1], (D_HIDDEN, D_MODEL), jnp.float32, -lim1, lim1), 'conv_w': jax.random.uniform(ks[2], (D_HIDDEN, 1, 3), jnp.float32, -limc, limc), 'conv_b': jax.random.uniform(ks[3], (D_HIDDEN,), jnp.float32, -limc, limc), 'w2': jax.random.uniform(ks[4], (D_MODEL, D_HIDDEN), jnp.float32, -lim2, lim2)}
    _L3_ffn_all = _L3_ffn_setup()
    _L3_ffn_in = {k: v for k, v in _L3_ffn_all.items() if k in ('w1', 'conv_w', 'conv_b', 'w2')}
    del _L3_ffn_all
    return {'x': x, 'ctx_2048': ctx_2048, 'mask_BxS2_fk1': mask_BxS2_fk1, 'mask_BxS2_if0': mask_BxS2_if0, 'mask_BxS2_ik0': mask_BxS2_ik0, 'g_xattn': g_xattn, 'g_ffn': g_ffn, 'L0_xattn_W_src': _L0_xattn_in['W_src'], 'L0_xattn_b_src': _L0_xattn_in['b_src'], 'L0_xattn_W_tgt': _L0_xattn_in['W_tgt'], 'L0_xattn_b_tgt': _L0_xattn_in['b_tgt'], 'L0_xattn_W_out': _L0_xattn_in['W_out'], 'L0_xattn_b_out': _L0_xattn_in['b_out'], 'L0_ffn_wqkv': _L0_ffn_in['wqkv'], 'L0_ffn_q_scale': _L0_ffn_in['q_scale'], 'L0_ffn_k_scale': _L0_ffn_in['k_scale'], 'L0_ffn_wo': _L0_ffn_in['wo'], 'L0_ffn_ln_g': _L0_ffn_in['ln_g'], 'L0_ffn_ln_b': _L0_ffn_in['ln_b'], 'L0_ffn_w1': _L0_ffn_in['w1'], 'L0_ffn_b1': _L0_ffn_in['b1'], 'L0_ffn_w2': _L0_ffn_in['w2'], 'L0_ffn_b2': _L0_ffn_in['b2'], 'L1_xattn_W_in': _L1_xattn_in['W_in'], 'L1_xattn_b_in': _L1_xattn_in['b_in'], 'L1_xattn_g_res': _L1_xattn_in['g_res'], 'L1_xattn_g_init': _L1_xattn_in['g_init'], 'L1_ffn_Wg': _L1_ffn_in['Wg'], 'L1_ffn_A': _L1_ffn_in['A'], 'L1_ffn_B': _L1_ffn_in['B'], 'L2_xattn_b': _L2_xattn_in['b'], 'L2_ffn_W1': _L2_ffn_in['W1'], 'L2_ffn_b1': _L2_ffn_in['b1'], 'L2_ffn_W2': _L2_ffn_in['W2'], 'L2_ffn_b2': _L2_ffn_in['b2'], 'L3_xattn_w_qkv': _L3_xattn_in['w_qkv'], 'L3_xattn_w_proj': _L3_xattn_in['w_proj'], 'L3_xattn_b_proj': _L3_xattn_in['b_proj'], 'L3_ffn_w1': _L3_ffn_in['w1'], 'L3_ffn_conv_w': _L3_ffn_in['conv_w'], 'L3_ffn_conv_b': _L3_ffn_in['conv_b'], 'L3_ffn_w2': _L3_ffn_in['w2']}

def reference(x, ctx_2048, mask_BxS2_fk1, mask_BxS2_if0, mask_BxS2_ik0, g_xattn, g_ffn, L0_xattn_W_src, L0_xattn_b_src, L0_xattn_W_tgt, L0_xattn_b_tgt, L0_xattn_W_out, L0_xattn_b_out, L0_ffn_wqkv, L0_ffn_q_scale, L0_ffn_k_scale, L0_ffn_wo, L0_ffn_ln_g, L0_ffn_ln_b, L0_ffn_w1, L0_ffn_b1, L0_ffn_w2, L0_ffn_b2, L1_xattn_W_in, L1_xattn_b_in, L1_xattn_g_res, L1_xattn_g_init, L1_ffn_Wg, L1_ffn_A, L1_ffn_B, L2_xattn_b, L2_ffn_W1, L2_ffn_b1, L2_ffn_W2, L2_ffn_b2, L3_xattn_w_qkv, L3_xattn_w_proj, L3_xattn_b_proj, L3_ffn_w1, L3_ffn_conv_w, L3_ffn_conv_b, L3_ffn_w2):
    import jax
    import jax.numpy as jnp

    def _L0_xattn_ref(src, tgt, src_mask, tgt_mask, W_src, b_src, W_tgt, b_tgt, W_out, b_out):
        import jax, jax.numpy as jnp
        import numpy as np
        B, S, T = (32, 64, 64)
        SRC_SIZE, TGT_SIZE, OUT_SIZE, NUM_HEAD = (256, 128, 128, 8)
        HEAD_DIM = OUT_SIZE // NUM_HEAD
        b, s, _ = src.shape
        t = tgt.shape[1]
        src_trans = jnp.einsum('bsf,of->bso', src, W_src) + b_src
        tgt_trans = jnp.einsum('btf,of->bto', tgt, W_tgt) + b_tgt
        src_trans = src_trans * src_mask[:, :, None]
        tgt_trans = tgt_trans * tgt_mask[:, :, None]
        src_key, src_val = jnp.split(src_trans, 2, axis=2)
        k = src_key.reshape(b, s, NUM_HEAD, HEAD_DIM)
        v = src_val.reshape(b, s, NUM_HEAD, HEAD_DIM)
        q = tgt_trans.reshape(b, t, NUM_HEAD, HEAD_DIM)
        scores = jnp.einsum('bthd,bshd->bhts', q, k) / np.sqrt(HEAD_DIM)
        scores = jnp.where(src_mask[:, None, None, :] == 0, -jnp.inf, scores)
        attn = jax.nn.softmax(scores, axis=-1)
        tgt_update = jnp.einsum('bhts,bshd->bthd', attn, v).reshape(b, t, OUT_SIZE)
        cat_tgt = jnp.concatenate([tgt, tgt_update], axis=2)
        return jnp.einsum('btf,of->bto', cat_tgt, W_out) + b_out

    def _L0_ffn_ref(x, wqkv, q_scale, k_scale, wo, ln_g, ln_b, w1, b1, w2, b2):
        import jax, jax.numpy as jnp
        import numpy as np
        DIM = 128
        DEPTH = 2
        HEADS = 8
        DIM_HEAD = 64
        WINDOW = 64
        INNER = HEADS * DIM_HEAD
        HID = int(DIM * 4 * 2 / 3)
        B, N = (2, 1024)
        QK_SCALE = 8.0

        def shift_token(t):
            t1, t2 = jnp.split(t, 2, axis=-1)
            t2 = jnp.pad(t2, ((0, 0), (1, 0), (0, 0)))[:, :-1]
            return jnp.concatenate([t1, t2], axis=-1)

        def l2norm(t):
            return t / jnp.clip(jnp.linalg.norm(t, axis=-1, keepdims=True), 1e-12)

        def rotate_half(x):
            x1, x2 = jnp.split(x, 2, axis=-1)
            return jnp.concatenate([-x2, x1], axis=-1)

        def rotary_xpos(q, k):
            n = q.shape[-2]
            half_idx = jnp.arange(0, DIM_HEAD, 2, dtype=jnp.float32)
            inv_freq = 1.0 / 10000.0 ** (half_idx / DIM_HEAD)
            t = jnp.arange(n, dtype=jnp.float32)
            freqs = t[:, None] * inv_freq[None, :]
            freqs = jnp.concatenate([freqs, freqs], axis=-1)
            base = (half_idx + 0.4 * DIM_HEAD) / (1.4 * DIM_HEAD)
            power = (t - n // 2) / float(WINDOW // 2)
            scale = base[None, :] ** power[:, None]
            scale = jnp.concatenate([scale, scale], axis=-1)
            cos, sin = (jnp.cos(freqs), jnp.sin(freqs))
            q = q * cos * scale + rotate_half(q) * sin * scale
            k = k * cos / scale + rotate_half(k) * sin / scale
            return (q, k)

        def local_attention(q, k, v):
            b, h, n, d = q.shape
            w = n // WINDOW
            bq = q.reshape(b, h, w, WINDOW, d) * QK_SCALE
            bk = k.reshape(b, h, w, WINDOW, d)
            bv = v.reshape(b, h, w, WINDOW, d)

            def look_around(t):
                p = jnp.pad(t, ((0, 0), (0, 0), (1, 0), (0, 0), (0, 0)))
                return jnp.concatenate([p[:, :, :w], p[:, :, 1:]], axis=3)
            bk, bv = (look_around(bk), look_around(bv))
            bt = jnp.arange(n).reshape(w, WINDOW)
            btp = jnp.pad(bt, ((1, 0), (0, 0)), constant_values=-1)
            btk = jnp.concatenate([btp[:w], btp[1:]], axis=1)
            sim = jnp.einsum('bhwid,bhwjd->bhwij', bq, bk)
            i = bt[:, :, None]
            j = btk[:, None, :]
            mask = (i < j) | (i > j + WINDOW) | (j == -1)
            sim = jnp.where(mask, -jnp.finfo(sim.dtype).max, sim)
            attn = jax.nn.softmax(sim, axis=-1)
            out = jnp.einsum('bhwij,bhwjd->bhwid', attn, bv)
            return out.reshape(b, h, n, d)

        def _layer(x, wqkv, qs, ksc, wo, lg, lb, w1, b1, w2, b2):
            b, n, _ = x.shape
            h = shift_token(x)
            qkv = h @ wqkv
            q, k, v = jnp.split(qkv, 3, axis=-1)
            to_heads = lambda t: t.reshape(b, n, HEADS, DIM_HEAD).transpose(0, 2, 1, 3)
            q, k, v = (to_heads(q), to_heads(k), to_heads(v))
            q = l2norm(q) * qs
            k = l2norm(k) * ksc
            q, k = rotary_xpos(q, k)
            o = local_attention(q, k, v)
            o = o.transpose(0, 2, 1, 3).reshape(b, n, INNER)
            x = x + o @ wo
            h = shift_token(x)
            mu = h.mean(-1, keepdims=True)
            var = h.var(-1, keepdims=True)
            h = (h - mu) / jnp.sqrt(var + 1e-05) * lg + lb
            h = h @ w1 + b1
            a, g = jnp.split(h, 2, axis=-1)
            h = a * jax.nn.gelu(g, approximate=False)
            x = x + h @ w2 + b2
            return x
        for l in range(DEPTH):
            x = _layer(x, wqkv[l], q_scale[l], k_scale[l], wo[l], ln_g[l], ln_b[l], w1[l], b1[l], w2[l], b2[l])
        return x

    def _L1_xattn_ref(embeds, patch_embeds, patch_lens, W_in, b_in, g_res, g_init):
        import jax, jax.numpy as jnp
        import numpy as np
        B, L, P = (4, 512, 128)
        D_MODEL = 128
        D_GLOBAL = 256
        HEADDIM = 32
        EPSILON = 0.001
        RMS_EPS = 1e-05

        def rmsnorm(x, g, eps=RMS_EPS):
            var = jnp.mean(jnp.square(x), axis=-1, keepdims=True)
            return x * jax.lax.rsqrt(var + eps) * g

        def _hnet_depool(h, h_patch_full, patch_lens):
            h_patch = h_patch_full[..., :D_MODEL]
            bsz, plen = (h_patch.shape[0], h_patch.shape[1])
            seqlen = h.shape[1]
            logp = jnp.full((bsz, plen), -EPSILON, dtype=jnp.float32)
            bidx = jnp.cumsum(patch_lens, axis=1) - 1
            boundary_mask = jnp.zeros((bsz, seqlen), dtype=jnp.int32)
            boundary_mask = boundary_mask.at[jnp.arange(bsz)[:, None], bidx].set(1)
            dt = (-jnp.log(-jnp.expm1(logp))).astype(h_patch.dtype)
            x = h_patch / dt[..., None]
            n_heads = D_MODEL // HEADDIM
            A = -jnp.ones((n_heads,), dtype=jnp.float32)
            bcoef = jnp.exp(logp).astype(h_patch.dtype)
            x4 = x.reshape(bsz, plen, n_heads, HEADDIM)
            a = jnp.exp(dt[:, :, None] * A[None, None, :])
            u = (dt * bcoef)[:, :, None, None] * x4
            a_b = jnp.broadcast_to(a[..., None], u.shape)

            def comb(lft, rgt):
                aL, uL = lft
                aR, uR = rgt
                return (aL * aR, uL * aR + uR)
            _, s = jax.lax.associative_scan(comb, (a_b, u), axis=1)
            depool = s.reshape(bsz, plen, D_MODEL)
            plug = jnp.clip(jnp.cumsum(boundary_mask, axis=1) - 1, 0, plen - 1)
            depool_out = depool[jnp.arange(bsz)[:, None], plug]
            return depool_out + h
        h = rmsnorm(embeds, g_res)
        h = jnp.einsum('bld,ed->ble', h, W_in) + b_in
        h_patch = rmsnorm(patch_embeds, g_init)
        return _hnet_depool(h, h_patch, patch_lens)

    def _L1_ffn_ref(x, Wg, A, B):
        import jax, jax.numpy as jnp
        import numpy as np
        TOP_K = 2
        D = x.shape[-1]
        E = Wg.shape[-1]
        xs = x.reshape(-1, D)
        gate_logits = xs @ Wg
        topw, sel = jax.lax.top_k(gate_logits, TOP_K)
        topw = jax.nn.softmax(topw.astype(jnp.float32), axis=-1).astype(x.dtype)
        cw = jnp.sum(jax.nn.one_hot(sel, E, dtype=x.dtype) * topw[..., None], axis=1)
        h = jnp.einsum('td,edr->ter', xs, A)
        hw = h * cw[..., None]
        out = jnp.einsum('ter,erd->td', hw, B)
        return out.reshape(x.shape)

    def _L2_xattn_ref(memory, query, seq_mask, b):
        import jax, jax.numpy as jnp
        import numpy as np
        UNITS = 128
        NUM_HEADS = 8

        def _split_heads(x, n):
            B, S, D = x.shape
            return x.reshape(B, S, n, D // n).transpose(0, 2, 1, 3)
        H = NUM_HEADS
        depth = UNITS // H
        Q = _split_heads(query, H) * depth ** (-0.5)
        k_mem, v_mem = jnp.split(memory, 2, axis=2)
        K = _split_heads(k_mem, H)
        V = _split_heads(v_mem, H)
        logits = jnp.einsum('bhqd,bhkd->bhqk', Q, K) + b[0]
        mask = seq_mask.astype(jnp.float32)[:, None, None, :]
        logits = logits + -1e+30 * (1.0 - mask)
        weights = jax.nn.softmax(logits, axis=-1)
        out = jnp.einsum('bhqk,bhkd->bhqd', weights, V)
        B, _, S, _ = out.shape
        return out.transpose(0, 2, 1, 3).reshape(B, S, UNITS)

    def _L2_ffn_ref(x, W1, b1, W2, b2):
        import jax, jax.numpy as jnp
        import numpy as np
        QB = 127.0
        EPS = 1e-05

        def _ste(x, q):
            return x + jax.lax.stop_gradient(q - x)

        def bitlinear(x, W, b):
            w_scale = jnp.clip(jnp.mean(jnp.abs(W)), EPS, None)
            Wq = _ste(W, jnp.clip(jnp.round(W / w_scale), -1.0, 1.0) * w_scale)
            x_scale = jnp.clip(jnp.max(jnp.abs(x), axis=-1, keepdims=True), EPS, None)
            xq = _ste(x, jnp.clip(jnp.round(x * (QB / x_scale)), -QB - 1.0, QB) * (x_scale / QB))
            return jnp.einsum('bnd,hd->bnh', xq, Wq) + b
        h = bitlinear(x, W1, b1)
        h = jax.nn.gelu(h, approximate=False)
        return bitlinear(h, W2, b2)

    def _L3_xattn_ref(x, context, w_qkv, w_proj, b_proj):
        import jax, jax.numpy as jnp
        import numpy as np
        NUM_HEADS = 16
        B, N, C = x.shape
        H = NUM_HEADS
        D = C // H
        scale = D ** (-0.5)
        qkv = (x @ w_qkv.T).reshape(B, N, 3, H, D).transpose(2, 0, 3, 1, 4)
        q, k, v = (qkv[0], qkv[1], qkv[2])
        N_c = context.shape[1]
        kv = context.reshape(B, N_c, 2, H, D).transpose(2, 0, 3, 1, 4)
        extra_k, extra_v = (kv[0], kv[1])
        k = jnp.concatenate([extra_k, k], axis=2)
        v = jnp.concatenate([extra_v, v], axis=2)
        dtype = q.dtype
        attn = jnp.einsum('bhnd,bhmd->bhnm', q * scale, k).astype(jnp.float32)
        attn = jax.nn.softmax(attn, axis=-1).astype(dtype)
        out = jnp.einsum('bhnm,bhmd->bhnd', attn, v)
        out = out.transpose(0, 2, 1, 3).reshape(B, N, C)
        return out @ w_proj.T + b_proj

    def _L3_ffn_ref(x, w1, conv_w, conv_b, w2):
        import jax, jax.numpy as jnp
        import numpy as np
        B, S, D_MODEL, D_HIDDEN = (4, 256, 128, 512)

        def act_quant(x):
            scale = 127.0 / jnp.clip(jnp.max(jnp.abs(x), axis=-1, keepdims=True), 1e-05)
            return jnp.clip(jnp.round(x * scale), -128, 127) / scale

        def weight_quant(w):
            scale = 1.0 / jnp.clip(jnp.mean(jnp.abs(w)), 1e-05)
            return jnp.clip(jnp.round(w * scale), -1, 1) / scale

        def bit_linear(x, w):
            xq = x + jax.lax.stop_gradient(act_quant(x) - x)
            wq = w + jax.lax.stop_gradient(weight_quant(w) - w)
            return jnp.einsum('bsd,hd->bsh', xq, wq)

        def depthwise_conv1d(x_bcl, w, b):
            y = jax.lax.conv_general_dilated(x_bcl, w, window_strides=(1,), padding=[(1, 1)], dimension_numbers=('NCH', 'OIH', 'NCH'), feature_group_count=x_bcl.shape[1])
            return y + b[None, :, None]
        h = bit_linear(x, w1)
        h = depthwise_conv1d(h.transpose(0, 2, 1), conv_w, conv_b)
        h = h.transpose(0, 2, 1)
        h = jax.nn.silu(h)
        return bit_linear(h, w2)
    x = x + jnp.tanh(g_xattn[0]) * _L0_xattn_ref(ctx_2048, _layernorm(x, axis=-1), mask_BxS2_fk1, mask_BxS2_fk1, L0_xattn_W_src, L0_xattn_b_src, L0_xattn_W_tgt, L0_xattn_b_tgt, L0_xattn_W_out, L0_xattn_b_out)
    x = x + jnp.tanh(g_ffn[0]) * _L0_ffn_ref(_layernorm(x, axis=-1), L0_ffn_wqkv, L0_ffn_q_scale, L0_ffn_k_scale, L0_ffn_wo, L0_ffn_ln_g, L0_ffn_ln_b, L0_ffn_w1, L0_ffn_b1, L0_ffn_w2, L0_ffn_b2)
    x = x + jnp.tanh(g_xattn[1]) * _L1_xattn_ref(_layernorm(x, axis=-1), ctx_2048, mask_BxS2_if0, L1_xattn_W_in, L1_xattn_b_in, L1_xattn_g_res, L1_xattn_g_init)
    x = x + jnp.tanh(g_ffn[1]) * _L1_ffn_ref(_layernorm(x, axis=-1), L1_ffn_Wg, L1_ffn_A, L1_ffn_B)
    x = x + jnp.tanh(g_xattn[2]) * _L2_xattn_ref(ctx_2048, _layernorm(x, axis=-1), mask_BxS2_ik0, L2_xattn_b)
    x = x + jnp.tanh(g_ffn[2]) * _L2_ffn_ref(_layernorm(x, axis=-1), L2_ffn_W1, L2_ffn_b1, L2_ffn_W2, L2_ffn_b2)
    x = x + jnp.tanh(g_xattn[3]) * _L3_xattn_ref(_layernorm(x, axis=-1), ctx_2048, L3_xattn_w_qkv, L3_xattn_w_proj, L3_xattn_b_proj)
    x = x + jnp.tanh(g_ffn[3]) * _L3_ffn_ref(_layernorm(x, axis=-1), L3_ffn_w1, L3_ffn_conv_w, L3_ffn_conv_b, L3_ffn_w2)
    return x

_drawn_inputs = setup_inputs


def setup_inputs(seed=0):
    import zlib

    import numpy as np

    out = dict(_drawn_inputs(seed))
    spreads = {'L0_xattn_b_src': (0.0, 0.488),
     'L0_xattn_b_tgt': (0.0, 0.8),
     'L0_xattn_b_out': (0.0, 0.279),
     'L0_ffn_q_scale': (1.0, 0.6),
     'L0_ffn_k_scale': (1.0, 0.6),
     'L0_ffn_ln_g': (1.0, 0.6),
     'L0_ffn_ln_b': (0.0, 0.8),
     'L0_ffn_b1': (0.0, 0.8),
     'L0_ffn_b2': (0.0, 0.1),
     'L1_xattn_b_in': (0.0, 0.359),
     'L1_xattn_g_res': (1.0, 0.6),
     'L1_xattn_g_init': (1.0, 0.2),
     'L2_ffn_b1': (0.0, 0.8),
     'L2_ffn_b2': (0.0, 0.397)}
    factors = {'g_ffn': 8.0,
     'L0_ffn_w1': 4.28,
     'L0_ffn_w2': 4.211,
     'L1_ffn_Wg': 6.688,
     'L1_ffn_A': 5.831,
     'L1_ffn_B': 5.811,
     'L2_ffn_W1': 3.95,
     'L2_ffn_W2': 3.307,
     'L3_xattn_w_qkv': 19.996,
     'L3_xattn_b_proj': 17.794,
     'L3_xattn_w_proj': 3.074,
     'L3_ffn_w1': 4.905,
     'L3_ffn_conv_w': 4.677,
     'L3_ffn_conv_b': 3.775,
     'L3_ffn_w2': 3.054}
    for name, (base, spread) in spreads.items():
        noise = np.random.default_rng([zlib.crc32(name.encode()), seed]).standard_normal(out[name].shape)
        drawn = base * np.exp(spread * noise) if base else spread * noise
        out[name] = jnp.asarray(drawn.astype(out[name].dtype))
    for name, factor in factors.items():
        out[name] = (out[name] * factor).astype(out[name].dtype)
    return out
```

```python
from contextlib import ExitStack
import math

import concourse.bass as bass
from concourse import mybir

ALU = mybir.AluOpType
ACT = mybir.ActivationFunctionType
AX = mybir.AxisListType
F32 = mybir.dt.float32
BF16 = mybir.dt.bfloat16
I32 = mybir.dt.int32

P = 128
D = 128
ROW = 64
B = 64
G = 4
TILES = B * ROW // P
PASSES = TILES // G
CTX = 256
HID = 512
INNER = 512
FF, FFC = 341, 3
E, R = 8, 16
LN_EPS = 1e-5
NEG = -1e30
ROUND = 1.5 * 2.0 ** 23
PATCH_EPS = 1e-3
PATCH_DT = -math.log(-math.expm1(-PATCH_EPS))
PATCH_B = math.exp(-PATCH_EPS)
BANK = 512

_LAYERS = ("l0f0", "l0f1")
_ATTENTIONS = ("l0a", "l0f0", "l0f1", "l2a", "l3a0", "l3a1")
_NORMS = ("l0a", "l0f", "l0f0", "l0f1", "l1a", "l1f", "l2a", "l2f", "l3a", "l3f")
_TERNARY = ("l2f", "l2g", "l3f", "l3g")
SHARED = {
    "var": _NORMS, "rstd": _NORMS, "y": _NORMS,
    "yt": ("l0a", "l0f0", "l0f1", "l1a", "l1f", "l2a", "l3a"),
    "ht": ("l0a", "l1a", "l1f", "l2a", "l3a"),
    "xb": ("l0a", "l1a", "l2f", "l3a"),
    "spread": ("l0a", "l2a", "l3a0", "l3a1"),
    "sc": _ATTENTIONS, "sub": _ATTENTIONS, "exp": _ATTENTIONS, "pt": _ATTENTIONS, "pv": _ATTENTIONS,
    "o": _ATTENTIONS, "pts": ("l0a", "l0f0", "l0f1", "l2a"), "ptsa": ("l3a0", "l3a1"), "ptsb": ("l3a0", "l3a1"),
    "ot": ("l0a", "l0f0", "l0f1", "l3a"), "ots": ("l0a", "l0f0", "l0f1", "l3a"),
    "out": ("l0a", "l0f0", "l0f1", "l1a", "l1f", "l2g", "l3a", "l3g"),
    "x": ("l0a", "l0f0", "l0f1", "l1a", "l1f", "l2g", "l3a"),
    "q": _TERNARY, "qt": _TERNARY, "qts": _LAYERS + _TERNARY,
    **{role: _LAYERS for role in ("ss", "rn", "turned", "rot", "hs", "qk", "sq", "v", "vs", "qkt", "kts", "qkn",
                                  "wo", "y1", "sh", "h2", "lt", "lts", "hid", "gelu", "gated", "yb")},
}


def place(name):
    block, _, role = name.partition("_")
    stages = SHARED.get(role, ())
    return (role, len(stages), stages.index(block)) if block in stages else (name, 1, 0)


def flamingo_stack(nc, d, out):
    ctx = ExitStack()
    with ctx:
        def sb(name, shape, dt=F32):
            return ctx.enter_context(nc.sbuf_tensor(name, shape, dt))

        semaphores = {}

        def sg(name):
            name = place(name)[0]
            if name not in semaphores:
                semaphores[name] = ctx.enter_context(nc.semaphore(name))
            return semaphores[name]

        def reached(name, it, n):
            _, stages, at = place(name)
            return it * (stages * G) + (at * G + n)

        def bc(ap, axis, n):
            shape = list(ap.shape)
            return ap.unsqueeze(axis).to_broadcast(shape[:axis] + [n] + shape[axis:])

        ident = sb("ident", [P, P])
        ident_bf = sb("ident_bf", [P, P], BF16)
        ones = sb("ones", [P, P])
        shift = sb("shift", [P, P])
        causal = sb("causal", [P, ROW])
        tri = sb("tri", [ROW, ROW])
        before = sb("before", [P, E, E])
        head8 = sb("head8", [P, 8])
        head16 = sb("head16", [P, 16])
        minus_half = sb("minus_half", [P, 64])
        patch_row = sb("patch_row", [P, 1])
        position = sb("position", [ROW, ROW])
        w_src = sb("w_src", [P, 2, 2 * D])
        w_tgt = sb("w_tgt", [P, D])
        w_out = sb("w_out", [P, 2, D])
        b_q = sb("b_q", [P, 1])
        b_k = sb("b_k", [P, 1])
        b_v = sb("b_v", [P, D])
        w_qkv = sb("w_qkv", [P, 2, 3 * INNER])
        w_o = sb("w_o", [P, 2, 4, D])
        w_1 = sb("w_1", [P, 2, 2, FFC, P])
        w_2 = sb("w_2", [P, 2, FFC, D])
        b_1 = sb("b_1", [P, 2, 2, FFC])
        b_2 = sb("b_2", [P, 2, D])
        ln_g = sb("ln_g", [P, 2])
        ln_b = sb("ln_b", [P, 2])
        qk_scale = sb("qk_scale", [P, 2, 2, ROW])
        rotary = sb("rotary", [P, 2, 2, ROW])
        turn = sb("turn", [P, 2, 2, 2, ROW])
        w_in = sb("w_in", [P, D])
        g_res = sb("g_res", [P, 1])
        g_init = sb("g_init", [P, D])
        w_gate = sb("w_gate", [P, E])
        w_a = sb("w_a", [P, E * R])
        w_b = sb("w_b", [P, D])
        logit_b = sb("logit_b", [P, 1])
        raw = sb("raw", [P, 4, HID])
        tern = sb("tern", [P, 4, HID], BF16)
        tern_sum = sb("tern_sum", [P, 4])
        tern_step = sb("tern_step", [P, 4])
        tern_inv = sb("tern_inv", [P, 4])
        tern_127 = sb("tern_127", [P, 4])
        b_t1 = sb("b_t1", [P, HID])
        w_qkv3 = sb("w_qkv3", [P, 3 * D])
        w_proj3 = sb("w_proj3", [P, D])
        conv_w = sb("conv_w", [P, 4, 3])
        conv_b = sb("conv_b", [P, 4])
        gate_in = sb("gate_in", [P, 8])
        gate = sb("gate", [P, 8])
        bias_in = sb("bias_in", [P, 4, D])
        bias = sb("bias", [P, 4, D])
        lens_i = sb("lens_i", [ROW, B], I32)
        lens = sb("lens", [ROW, B])
        last = sb("last", [B, ROW])
        wrap = sb("wrap", [B, ROW])
        bound = sb("bound", [B, ROW])
        bound_t = sb("bound_t", [ROW, B])
        plug_all = sb("plug_all", [B, ROW])

        xin = sb("xin", [P, G, D])
        x = sb("x", [P, G, D])
        ctx_s = sb("ctx_s", [P, G, CTX])
        ctx_t = sb("ctx_t", [P, G, 2, P])
        ctx_v = sb("ctx_v", [ROW, G, 2, D])
        mask_row = sb("mask_row", [P, G, P])
        mask_col = sb("mask_col", [P, G, 1])
        mask_i = sb("mask_i", [P, G, P], I32)
        plug = sb("plug", [P, G, ROW])
        neg0 = sb("neg0", [P, G, P])
        neg2 = sb("neg2", [P, G, P])
        stats = sb("stats", [P, G, 6])
        mv = sb("mv", [P, G, 2])
        var_eps = sb("var_eps", [P, G])
        rstd = sb("rstd", [P, G])
        small = sb("small", [P, G])
        small2 = sb("small2", [P, G])
        ctx_sq = sb("ctx_sq", [P, G])
        y = sb("y", [P, G, D])
        h = sb("h", [P, G, D])
        vtmp = sb("vtmp", [P, G, D])
        ht = sb("ht", [P, G, P])
        ht_shift = sb("ht_shift", [P, G, 2, ROW])
        qt = sb("qt", [P, G, P])
        kt = sb("kt", [P, G, P])
        k_cat = sb("k_cat", [P, G, 2, 2, ROW])
        v8 = sb("v8", [P, G, 8, 17])
        v16 = sb("v16", [P, G, 2, 16, 9])
        patches = sb("patches", [P, G, D])
        pick = sb("pick", [P, G, 2, ROW])
        decay = sb("decay", [P, G, ROW])
        reach = sb("reach", [P, G, ROW])
        mx = sb("mx", [P, G, 16])
        den = sb("den", [P, G, 16])
        rden = sb("rden", [P, G, 16])
        wide_a = sb("wide_a", [P, G, 2 * BANK])
        wide_b = sb("wide_b", [P, G, 2 * BANK])
        wide_c = sb("wide_c", [P, G, 2 * BANK])
        quant = sb("quant", [P, G, HID], BF16)
        quant_t = sb("quant_t", [P, G, HID], BF16)
        scale_t = sb("scale_t", [P, G, P])
        logits = sb("logits", [P, G, E])
        rank_a = sb("rank_a", [P, G, E, E])
        rank_b = sb("rank_b", [P, G, E, E])
        rank = sb("rank", [P, G, E])

        ps_all = ctx.enter_context(nc.psum_tensor("ps_all", [P, G, 2 * BANK], F32))
        plug_dram = nc.dram_tensor("plug_dram", [B, ROW], F32, kind="Internal").ap()

        def ps(s, a=0, n=2 * BANK):
            return ps_all[:, s, a:a + n]

        TS = range(G)
        TILE_IN = ("xin_in", "ctx_in", "ctxt_in", "ctxv_in", "maskr_in", "maski_in")
        TILE_LOADS = 16 * len(TILE_IN)

        once = [
            (w_src, d["w_src"]), (w_tgt, d["w_tgt"]), (w_out, d["w_out"]), (b_q, d["b_q"]), (b_k, d["b_k"]),
            (b_v, d["b_v"]), (w_qkv, d["w_qkv"]), (w_o, d["w_o"]), (b_2, d["b_2"]), (ln_g, d["ln_g"]),
            (ln_b, d["ln_b"]), (qk_scale, d["qk_scale"]), (rotary, d["rotary"]), (w_in, d["w_in"]),
            (g_res, d["g_res"]), (g_init, d["g_init"]), (w_gate, d["w_gate"]), (w_a, d["w_a"]), (w_b, d["w_b"]),
            (logit_b, d["logit_b"]), (raw, d["tern"]), (b_t1, d["b_t1"]), (w_qkv3, d["w_qkv3"]),
            (w_proj3, d["w_proj3"]), (conv_w, d["conv_w"]), (conv_b, d["conv_b"]), (gate_in, d["gate_in"]),
            (bias_in, d["bias_in"]), (w_1, d["w_1"]), (w_2, d["w_2"]), (b_1, d["b_1"]),
        ]

        def settle(eng, count):
            eng.sem_inc(sg(count), 1)

        block = ctx.enter_context(nc.Block())

        @block.sync
        def _(sp):
            def load(it, s, names):
                what = {
                    "xin_in": (xin[:, s, :], d["x"][it, s]),
                    "ctx_in": (ctx_s[:, s, :], d["ctx"][it, s]),
                    "ctxt_in": (ctx_t[:, s, :, :], d["ctx_t"][it, s]),
                    "ctxv_in": (ctx_v[:, s, :, :], d["ctx"][it, s, :, D:CTX].rearrange("(b t) f -> t b f", b=2)),
                    "maskr_in": (mask_row[:, s, :], d["mask_f"][it, s].partition_broadcast(P)),
                    "maskc_in": (mask_col[:, s, :], d["mask_f"][it, s].unsqueeze(1)),
                    "maski_in": (mask_i[:, s, :], d["mask_i"][it, s].partition_broadcast(P)),
                }
                for name in names:
                    to, of = what[name]
                    done = "maskc_in" if name == "maskc_in" else "tile_in"
                    sp.dma_start(to, of).then_inc(sg(f"{done}{s}"), 16)

            def load_plug(it, s):
                for b in range(2):
                    rows = plug_dram.rearrange("(i s b) l -> i s b l", s=G, b=2)[it, s, b]
                    sp.dma_start(plug[64 * b:64 * b + 64, s, :], rows.partition_broadcast(ROW)).then_inc(
                        sg(f"plug_in{s}"), 16)

            sp.dma_start(lens_i[:], d["lens_t"]).then_inc(sg("lens_in"), 16)
            for s in TS:
                load(0, s, TILE_IN + ("maskc_in",))
            for n, (to, of) in enumerate(once):
                sp.dma_start(to[:], of).then_inc(sg("weights_in"), 16)
            sp.wait_ge(sg("plug_made"), 1)
            sp.dma_start(plug_dram, plug_all[:]).then_inc(sg("plug_kept"), 16)
            sp.wait_ge(sg("plug_kept"), 16)
            for s in TS:
                load_plug(0, s)
            with sp.Fori(0, PASSES - 1) as it:
                for s in TS:
                    sp.wait_ge(sg("l3_ctx_used"), reached("l3_ctx_used", it, s + 1))
                    load(it + 1, s, TILE_IN)
                    load_plug(it + 1, s)
                for s in TS:
                    sp.wait_ge(sg("l3f_x"), reached("l3f_x", it, s + 1))
                    sp.dma_start(out[it, s], x[:, s, :]).then_inc(sg(f"stored{s}"), 16)
                for s in TS:
                    sp.wait_ge(sg(f"stored{s}"), it * 16 + 16)
                    load(it + 1, s, ("maskc_in",))
            for s in TS:
                sp.wait_ge(sg("l3f_x"), TILES - G + s + 1)
                sp.dma_start(out[PASSES - 1, s], x[:, s, :]).then_inc(sg(f"stored{s}"), 16)
            for s in TS:
                sp.wait_ge(sg(f"stored{s}"), 16 * PASSES)

        @block.gpsimd
        def _(pool):
            g = nc.gpsimd

            def tt(o, a, b, op):
                return g.tensor_tensor(o, a, b, op)

            g.memset(ident[:], 0.0)
            g.memset(shift[:], 0.0)
            g.memset(causal[:], 0.0)
            g.memset(tri[:], 1.0)
            g.memset(before[:], 1.0)
            g.memset(head8[:], 16.0 ** -0.5)
            g.memset(head16[:], 8.0 ** -0.5)
            g.memset(minus_half[:], -0.5)
            g.memset(ones[:], 1.0)
            g.drain()
            g.affine_select(out=ident[:], in_=ident[:], compare_op=ALU.not_equal, fill=1.0, base=0,
                            pattern=[[-1, P]], channel_multiplier=1)
            g.affine_select(out=shift[:], in_=shift[:], compare_op=ALU.not_equal, fill=1.0, base=-1,
                            pattern=[[1, P]], channel_multiplier=-1)
            for b in range(2):
                half = causal[64 * b:64 * b + 64, :]
                g.drain()
                g.affine_select(out=half, in_=half, compare_op=ALU.is_ge, fill=NEG, base=0,
                                pattern=[[-1, ROW]], channel_multiplier=1)
            g.drain()
            g.affine_select(out=tri[:], in_=tri[:], compare_op=ALU.is_ge, fill=0.0, base=0,
                            pattern=[[1, ROW]], channel_multiplier=-1)
            g.drain()
            g.affine_select(out=before[:], in_=before[:], compare_op=ALU.is_gt, fill=0.0, base=0,
                            pattern=[[1, E], [-1, E]], channel_multiplier=0)
            g.affine_select(out=head8[:], in_=head8[:], compare_op=ALU.is_ge, fill=0.0, base=0,
                            pattern=[[-16, 8]], channel_multiplier=1)
            g.affine_select(out=head16[:], in_=head16[:], compare_op=ALU.is_ge, fill=0.0, base=0,
                            pattern=[[-8, 16]], channel_multiplier=1)
            g.iota(position[:], pattern=[[1, ROW]], base=0, channel_multiplier=0,
                   allow_small_or_imprecise_dtypes=True)
            for b in range(2):
                g.drain()
                g.iota(patch_row[64 * b:64 * b + 64, :], pattern=[[0, 1]], base=0, channel_multiplier=1,
                       allow_small_or_imprecise_dtypes=True)
            g.drain()
            g.affine_select(out=head8[:], in_=head8[:], compare_op=ALU.is_ge, fill=0.0, base=15,
                            pattern=[[16, 8]], channel_multiplier=-1)
            g.affine_select(out=head16[:], in_=head16[:], compare_op=ALU.is_ge, fill=0.0, base=7,
                            pattern=[[8, 16]], channel_multiplier=-1)
            g.memset(shift[:, 64:65], 0.0)
            g.tensor_copy(ident_bf[:], ident[:])
            g.memset(ht_shift[:], 0.0)
            g.memset(v8[:], 1.0)
            g.memset(v16[:], 1.0)
            g.memset(pick[:], 0.0)
            g.drain().then_inc(sg("consts"), 1)

            with pool.Fori(0, PASSES) as it:

                def tile(name, s):
                    pool.wait_ge(sg(name), reached(name, it, s + 1))

                def tiles(name):
                    pool.wait_ge(sg(name), reached(name, it, G))

                def inv_root(o, i, wait, done):
                    tiles(wait)
                    g.tensor_tensor(o, i, minus_half[:, 0:o.free_size()] if len(o.shape) == 2 else
                                    minus_half[:, 0:o.free_size()].rearrange("p (a b) -> p a b", a=G),
                                    ALU.pow).then_inc(sg(done), G)

                def residual_bias(n, name_ready, name_done, of):
                    for s in TS:
                        tile(name_ready, s)
                        tt(x[:, s, :], of[:, s, :], bias[:, n, :], ALU.add).then_inc(sg(name_done), 1)

                def spread_heads(src, table, heads, wait, done, row=None):
                    for s in TS:
                        tile(wait, s)
                        if row is None:
                            to = wide_a[:, s, :].rearrange("p (b h t) -> p b h t", b=2, h=heads)
                            for b in range(2):
                                i = tt(to[:, b], bc(src[:, s, 64 * b:64 * b + 64], 1, heads),
                                       bc(table[:], 2, ROW), ALU.mult)
                            i.then_inc(sg(done), 1)
                        else:
                            to = wide_a[:, s, :].rearrange("p (h t) -> p h t", h=heads)
                            tt(to, bc(src[:, s, 64 * row:64 * row + 64], 1, heads),
                               bc(table[:], 2, ROW), ALU.mult).then_inc(sg(done), 1)

                for s in TS:
                    pool.wait_ge(sg(f"tile_in{s}"), (it + 1) * TILE_LOADS)
                    settle(pool, "pool_waits")
                    g.tensor_scalar(neg0[:, s, :], mask_row[:, s, :], 0.0, NEG, ALU.is_equal, ALU.mult
                                    ).then_inc(sg("l0a_neg"), 1)
                inv_root(rstd[:], var_eps[:], "l0a_var", "l0a_rstd")
                for s in TS:
                    pool.wait_ge(sg(f"tile_in{s}"), (it + 1) * TILE_LOADS)
                    settle(pool, "pool_waits")
                    g.tensor_scalar(neg2[:, s, :], mask_i[:, s, :], -1.0, 1.0, ALU.mult, ALU.add)
                g.drain()
                for s in TS:
                    g.tensor_scalar(neg2[:, s, :], neg2[:, s, :], NEG, None, ALU.mult)
                g.drain()
                pool.wait_ge(sg("setup_dve"), 1)
                for s in TS:
                    g.tensor_scalar(neg2[:, s, :], neg2[:, s, :], logit_b[:, 0:1], None, ALU.add
                                    ).then_inc(sg("l2a_neg"), 1)
                inv_root(ctx_sq[:], ctx_sq[:], "patch_ms", "patch_rms")
                for s in TS:
                    pool.wait_ge(sg(f"maskc_in{s}"), it * 16 + 16)
                residual_bias(0, "l0a_y", "l0a_xb", xin)
                spread_heads(qt, head8, 8, "l0a_qk", "l0a_spread")
                inv_root(rstd[:], var_eps[:], "l0f_var", "l0f_rstd")
                for L in range(2):
                    n = f"l0f{L}"
                    inv_root(rden[:], den[:], f"{n}_ss", f"{n}_rn")
                    for s in TS:
                        tile(f"{n}_turned", s)
                        tt(wide_a[:, s, :], wide_a[:, s, :], wide_b[:, s, :], ALU.add).then_inc(sg(f"{n}_rot"), 1)
                    inv_root(rstd[:], var_eps[:], f"{n}_var", f"{n}_rstd")
                    for s in TS:
                        tile(f"{n}_y", s)
                        tt(y[:, s, :], y[:, s, :], b_2[:, L, :], ALU.add).then_inc(sg(f"{n}_yb"), 1)
                inv_root(rstd[:], var_eps[:], "l1a_var", "l1a_rstd")
                inv_root(small2[:], small[:], "l1a_ms", "l1a_rms")
                residual_bias(1, "l1a_y", "l1a_xb", x)
                inv_root(rstd[:], var_eps[:], "l1f_var", "l1f_rstd")
                for s in TS:
                    g.tensor_copy(v8[:, s, :, 0:16],
                                  ctx_s[:, s, D:CTX].rearrange("p (h e) -> p h e", h=8)).then_inc(sg("l2a_v"), 1)
                inv_root(rstd[:], var_eps[:], "l2a_var", "l2a_rstd")
                spread_heads(ht, head8, 8, "l2a_ht", "l2a_spread")
                for s in TS:
                    for b in range(2):
                        g.tensor_copy(k_cat[:, s, b, 0, :], ctx_t[:, s, 0, 64 * b:64 * b + 64])
                g.drain()
                for s in TS:
                    for b in range(2):
                        i = g.tensor_copy(v16[0:64, s, b, :, 0:8],
                                          ctx_v[:, s, b, :].rearrange("p (h e) -> p h e", h=16))
                    i.then_inc(sg("l3_ctx"), 1)
                g.drain()
                for s in TS:
                    tile("l2a_o", s)
                    pool.sem_inc(sg("l3_ctx_used"), 1)
                inv_root(rstd[:], var_eps[:], "l2f_var", "l2f_rstd")
                residual_bias(2, "l2f_y", "l2f_xb", x)
                inv_root(rstd[:], var_eps[:], "l3a_var", "l3a_rstd")
                residual_bias(3, "l3a_y", "l3a_xb", x)
                for b in range(2):
                    spread_heads(qt, head16, 16, ("l3a_qk", "l3a0_pv")[b], f"l3a{b}_spread", row=b)
                inv_root(rstd[:], var_eps[:], "l3f_var", "l3f_rstd")

        @block.scalar
        def _(act):
            a = nc.scalar
            act.wait_ge(sg("weights_in"), 16 * len(once))
            a.activation(gate[:], gate_in[:], ACT.Tanh).then_inc(sg("gates"), 1)

            with act.Fori(0, PASSES) as it:

                def tile(name, s):
                    act.wait_ge(sg(name), reached(name, it, s + 1))

                def move(wait, done, to, of):
                    for s in TS:
                        tile(wait, s)
                        a.copy(to(s), of(s)).then_inc(sg(done), 1)

                def exps(n, width):
                    for s in TS:
                        tile(f"{n}_sub", s)
                        a.activation(wide_b[:, s, 0:width], wide_b[:, s, 0:width], ACT.Exp).then_inc(
                            sg(f"{n}_exp"), 1)

                for s in TS:
                    act.wait_ge(sg(f"tile_in{s}"), (it + 1) * TILE_LOADS)
                    a.activation(wide_c[:, s, 0:CTX], ctx_s[:, s, :], ACT.Square,
                                 accum_out=ctx_sq[:, s:s + 1]).then_inc(sg("patch_sq"), 1)
                move("l0a_yt", "l0a_ht", lambda s: ht[:, s, :], lambda s: ps(s, 0, P))
                exps("l0a", BANK)
                move("l0a_pt", "l0a_pts", lambda s: wide_c[:, s, 0:BANK], lambda s: ps(s, BANK, BANK))
                move("l0a_ot", "l0a_ots", lambda s: qt[:, s, :], lambda s: ps(s, 0, P))
                for L in range(2):
                    n = f"l0f{L}"
                    for s in TS:
                        tile(f"{n}_yt", s)
                        a.copy(ht_shift[0:64, s, :, :], ps(s, 0, P)[0:64].rearrange("p (b t) -> p b t", b=2))
                        a.copy(ht_shift[64:128, s, :, 1:ROW],
                               ps(s, 0, P)[64:128].rearrange("p (b t) -> p b t", b=2)[:, :, 0:ROW - 1]
                               ).then_inc(sg(f"{n}_hs"), 1)
                    for s in TS:
                        tile(f"{n}_qk", s)
                        a.activation(wide_c[:, s, :], ps(s), ACT.Square).then_inc(sg(f"{n}_sq"), 1)
                    for s in TS:
                        tile(f"{n}_v", s)
                        a.copy(wide_c[:, s, :], ps(s)).then_inc(sg(f"{n}_vs"), 1)
                    move(f"{n}_qkt", f"{n}_qts", lambda s: wide_a[:, s, 0:BANK], lambda s: ps(s, 0, BANK))
                    exps(n, BANK)
                    move(f"{n}_pt", f"{n}_pts", lambda s: wide_a[:, s, 0:BANK], lambda s: ps(s, 0, BANK))
                    move(f"{n}_ot", f"{n}_ots", lambda s: wide_a[:, s, 0:BANK], lambda s: ps(s, 0, BANK))
                    move(f"{n}_sh", f"{n}_h2", lambda s: h[:, s, 64:128], lambda s: ps(s, 0, 64))
                    for s in TS:
                        tile(f"{n}_lt", s)
                        a.activation(ht[:, s, :], ps(s, 0, P), ACT.Identity, scale=ln_g[:, L:L + 1],
                                     bias=ln_b[:, L:L + 1]).then_inc(sg(f"{n}_lts"), 1)
                    for s in TS:
                        tile(f"{n}_hid", s)
                        for c in range(FFC):
                            i = a.activation(wide_b[:, s, c * P:c * P + P], ps(s, BANK + c * P, P), ACT.Gelu,
                                             bias=b_1[:, L, 1, c:c + 1])
                        i.then_inc(sg(f"{n}_gelu"), 1)
                for s in TS:
                    tile("l1a_decay", s)
                    a.activation(decay[:, s, :], decay[:, s, :], ACT.Exp, scale=-PATCH_DT).then_inc(
                        sg("l1a_power"), 1)
                move("l1a_yt", "l1a_ht", lambda s: ht[:, s, :], lambda s: ps(s, 0, P))
                move("l1f_yt", "l1f_ht", lambda s: ht[:, s, :], lambda s: ps(s, 0, P))
                act.wait_ge(sg("l1f_less"), reached("l1f_less", it, G))
                a.activation(rank_b[:, :, 0, :], logits[:], ACT.Exp).then_inc(sg("l1f_exp"), G)
                move("l1f_hwt", "l1f_hwts", lambda s: ht[:, s, :], lambda s: ps(s, 0, P))
                move("l2a_yt", "l2a_ht", lambda s: ht[:, s, :], lambda s: ps(s, 0, P))
                exps("l2a", BANK)
                move("l2a_pt", "l2a_pts", lambda s: wide_c[:, s, 0:BANK], lambda s: ps(s, BANK, BANK))

                def quantised(n, k):
                    for s in TS:
                        tile(f"{n}_qt", s)
                        a.copy(quant_t[:, s, 0:k * P], ps(s, 0, k * P // 2).bitcast(BF16)).then_inc(
                            sg(f"{n}_qts"), 1)

                quantised("l2f", 1)
                for s in TS:
                    tile("l2f_pre", s)
                    a.activation(wide_b[:, s, 0:HID], wide_a[:, s, 0:HID], ACT.Gelu).then_inc(sg("l2f_gelu"), 1)
                quantised("l2g", 4)
                move("l3a_yt", "l3a_ht", lambda s: ht[:, s, :], lambda s: ps(s, 0, P))
                for s in TS:
                    tile("l3a_qkv", s)
                    a.copy(qt[:, s, :], ps(s, 0, P))
                    a.copy(k_cat[:, s, :, 1, :], ps(s, P, P).rearrange("p (b t) -> p b t", b=2)).then_inc(
                        sg("l3a_qk"), 1)
                for b in range(2):
                    exps(f"l3a{b}", 2 * BANK)
                    move(f"l3a{b}_pt", f"l3a{b}_ptsa", lambda s: wide_c[:, s, 0:BANK], lambda s: ps(s, 0, BANK))
                move("l3a_ot", "l3a_ots", lambda s: qt[:, s, :], lambda s: ps(s, 0, P))
                quantised("l3f", 1)
                move("l3f_st", "l3f_sts", lambda s: scale_t[:, s, :], lambda s: ps(s, BANK, P))
                for s in TS:
                    tile("l3f_conv", s)
                    a.activation(wide_b[:, s, 0:HID], wide_b[:, s, 0:HID], ACT.Silu).then_inc(sg("l3f_silu"), 1)
                quantised("l3g", 4)

        @block.vector
        def _(dve):
            v = nc.vector
            tt, ts, stt = v.tensor_tensor, v.tensor_scalar, v.scalar_tensor_tensor

            dve.wait_ge(sg("lens_in"), 16)
            v.tensor_copy(lens[:], lens_i[:]).then_inc(sg("lens_f"), 1)
            dve.wait_ge(sg("cum"), 1)
            dve.wait_ge(sg("consts"), 1)
            ts(last[:], ps(0, 0, ROW)[0:B], -1.0, None, ALU.add)
            v.drain()
            ts(wrap[:], last[:], 0.0, float(ROW), ALU.is_lt, ALU.mult)
            v.drain()
            tt(last[:], last[:], wrap[:], ALU.add)
            v.drain()
            hit = wide_a[0:B, :, :].rearrange("p g w -> p (g w)").rearrange("p (l j) -> p l j", l=ROW)
            tt(hit, bc(last[:], 1, ROW), bc(position[:], 2, ROW), ALU.is_equal)
            v.drain()
            v.tensor_reduce(bound[:], hit, AX.X, ALU.max).then_inc(sg("bound"), 1)
            dve.wait_ge(sg("bound_tp"), 1)
            v.tensor_copy(bound_t[:], ps(0, 0, B)[0:ROW]).then_inc(sg("bound_ts"), 1)
            dve.wait_ge(sg("plug_p"), 1)
            ts(plug_all[:], ps(0, 0, ROW)[0:B], -1.0, 0.0, ALU.add, ALU.max)
            v.drain().then_inc(sg("plug_made"), 1)

            dve.wait_ge(sg("weights_in"), 16 * len(once))
            dve.wait_ge(sg("gates"), 1)
            for n, of in enumerate((0, 1, 6, 3)):
                ts(bias[:, n, :], bias_in[:, n, :], gate[:, of:of + 1], None, ALU.mult)
            ts(w_in[:], w_in[:], g_res[:, 0:1], None, ALU.mult)
            for L in range(2):
                for qk in range(2):
                    tt(turn[:, L, qk, 0, :], rotary[:, qk, 0, :], qk_scale[:, L, qk, :], ALU.mult)
                    for half in range(2):
                        tt(turn[:, L, qk, 1, 32 * half:32 * half + 32],
                           rotary[:, qk, 1, 32 * half:32 * half + 32],
                           qk_scale[:, L, qk, 32 - 32 * half:64 - 32 * half], ALU.mult)
            v.tensor_reduce(tern_sum[:], raw[:], AX.X, ALU.add, apply_absolute_value=True)
            v.drain().then_inc(sg("tern_rows"), 1)
            dve.wait_ge(sg("tern_all"), 1)
            ts(tern_step[:], ps(0, 0, 4), 1.0 / (P * HID), LN_EPS, ALU.mult, ALU.max)
            v.drain()
            v.reciprocal(tern_inv[:], tern_step[:])
            ts(tern_127[:], tern_step[:], 1.0 / 127.0, None, ALU.mult)
            v.drain()
            for n in range(4):
                ts(raw[:, n, :], raw[:, n, :], tern_inv[:, n:n + 1], ROUND, ALU.mult, ALU.add)
            v.drain()
            for n in range(4):
                ts(raw[:, n, :], raw[:, n, :], -ROUND, 1.0, ALU.add, ALU.min)
            v.drain()
            for n in range(4):
                ts(tern[:, n, :], raw[:, n, :], -1.0, None, ALU.max)
            v.drain().then_inc(sg("setup_dve"), 1)

            with dve.Fori(0, PASSES) as it:

                def tile(name, s):
                    dve.wait_ge(sg(name), reached(name, it, s + 1))

                def tiles(name):
                    dve.wait_ge(sg(name), reached(name, it, G))

                def statistics(n, of):
                    for s in TS:
                        v.bn_stats(stats[:, s, :], of[:, s, :])
                    v.drain()
                    for s in TS:
                        v.bn_aggr(mv[:, s, :], stats[:, s, :])
                    v.drain()
                    ts(var_eps[:], mv[:, :, 1], LN_EPS, None, ALU.add).then_inc(sg(f"{n}_var"), G)

                def normalise(n, to, of, by=None):
                    by = rstd if by is None else by
                    for s in TS:
                        ts(to[:, s, :], of[:, s, :], mv[:, s, 0:1], by[:, s:s + 1], ALU.subtract, ALU.mult
                           ).then_inc(sg(f"{n}_y"), 1)

                def layer_norm(n, of=x):
                    v.drain()
                    statistics(n, of)
                    tiles(f"{n}_rstd")
                    normalise(n, y, of)

                def softmax_less_max(n, of, groups, neg=None):
                    for s in TS:
                        tile(f"{n}_sc", s)
                        if neg is not None:
                            neg(s)
                    if neg is not None:
                        v.drain()
                    for s in TS:
                        v.tensor_reduce(mx[:, s, 0:groups], of(s), AX.X, ALU.max)
                    v.drain()
                    for s in TS:
                        o = of(s)
                        to = wide_b[:, s, 0:groups * o.shape[2]].rearrange("p (g k) -> p g k", g=groups)
                        tt(to, o, bc(mx[:, s, 0:groups], 2, o.shape[2]), ALU.subtract).then_inc(sg(f"{n}_sub"), 1)

                def grouped(s, groups, keys):
                    return wide_b[:, s, 0:groups * keys].rearrange("p (g k) -> p g k", g=groups)

                def divide_heads(n, to):
                    def part(s, b):
                        return ps(s, b * BANK, 8 * 17)[64 * b:64 * b + 64].rearrange("p (h e) -> p h e", h=8)
                    for s in TS:
                        tile(f"{n}_pv", s)
                        for b in range(2):
                            v.reciprocal(rden[64 * b:64 * b + 64, s, 0:8], part(s, b)[:, :, 16])
                    v.drain()
                    for s in TS:
                        for b in range(2):
                            i = tt(to[64 * b:64 * b + 64, s, :].rearrange("p (h e) -> p h e", h=8),
                                   part(s, b)[:, :, 0:16],
                                   bc(rden[64 * b:64 * b + 64, s, 0:8], 2, 16), ALU.mult)
                        i.then_inc(sg(f"{n}_o"), 1)

                def update(n, col, at, bias_done=None):
                    for s in TS:
                        tile(f"{n}_out", s)
                        if bias_done:
                            tile(bias_done, s)
                        stt(x[:, s, :], ps(s, at, D), gate[:, col:col + 1], x[:, s, :], ALU.mult, ALU.add
                            ).then_inc(sg(f"{n}_x"), 1)

                for s in TS:
                    dve.wait_ge(sg(f"tile_in{s}"), (it + 1) * TILE_LOADS)
                statistics("l0a", xin)
                tiles("patch_sq")
                v.tensor_scalar(ctx_sq[:], ctx_sq[:], 1.0 / CTX, LN_EPS, ALU.mult, ALU.add).then_inc(
                    sg("patch_ms"), G)
                tiles("l0a_rstd")
                normalise("l0a", y, xin)
                for s in TS:
                    tile("l0a_qkv", s)
                    dve.wait_ge(sg(f"tile_in{s}"), (it + 1) * TILE_LOADS)
                    dve.wait_ge(sg(f"maskc_in{s}"), it * 16 + 16)
                    stt(qt[:, s, :], ps(s, 0, P), b_q[:, 0:1], mask_row[:, s, :], ALU.add, ALU.mult)
                    stt(kt[:, s, :], ps(s, P, P), b_k[:, 0:1], mask_row[:, s, :], ALU.add, ALU.mult
                        ).then_inc(sg("l0a_qk"), 1)
                    tt(vtmp[:, s, :], ps(s, BANK, D), b_v[:], ALU.add)
                v.drain()
                for s in TS:
                    ts(v8[:, s, :, 0:16], vtmp[:, s, :].rearrange("p (h e) -> p h e", h=8), mask_col[:, s, :],
                       None, ALU.mult).then_inc(sg("l0a_v"), 1)
                tiles("patch_rms")
                for s in TS:
                    stt(patches[:, s, :], ctx_s[:, s, 0:D], ctx_sq[:, s:s + 1], g_init[:], ALU.mult, ALU.mult
                        ).then_inc(sg("patches"), 1)

                def add_neg(neg):
                    def go(s):
                        tt(wide_b[:, s, 0:BANK].rearrange("p (g k) -> p g k", g=4),
                           ps(s, 0, BANK).rearrange("p (g k) -> p g k", g=4), bc(neg[:, s, :], 1, 4), ALU.add)
                    return go

                tiles("l0a_neg")
                softmax_less_max("l0a", lambda s: grouped(s, 8, ROW), 8, add_neg(neg0))
                divide_heads("l0a", vtmp)
                update("l0a", 0, BANK, "l0a_xb")

                layer_norm("l0f")
                for L in range(2):
                    n = f"l0f{L}"
                    for s in TS:
                        tile(f"{n}_sq", s)
                        v.tensor_reduce(den[:, s, :], wide_c[:, s, :].rearrange("p (g e) -> p g e", g=16),
                                        AX.X, ALU.add)
                        src = ps(s).rearrange("p (q h e) -> p q h e", q=2, h=8)
                        cos = wide_a[:, s, :].rearrange("p (q h e) -> p q h e", q=2, h=8)
                        sin = wide_b[:, s, :].rearrange("p (q h e) -> p q h e", q=2, h=8)
                        for q in range(2):
                            tt(cos[:, q], src[:, q], bc(turn[:, L, q, 0, :], 1, 8), ALU.mult)
                            for half in range(2):
                                lo, hi = 32 * half, 32 - 32 * half
                                i = tt(sin[:, q, :, lo:lo + 32], src[:, q, :, hi:hi + 32],
                                       bc(turn[:, L, q, 1, lo:lo + 32], 1, 8), ALU.mult)
                        i.then_inc(sg(f"{n}_turned"), 1)
                    v.drain()
                    ts(den[:], den[:], 1e-24, None, ALU.max).then_inc(sg(f"{n}_ss"), G)
                    tiles(f"{n}_rn")
                    for s in TS:
                        tile(f"{n}_rot", s)
                        tt(wide_b[:, s, :].rearrange("p (g e) -> p g e", g=16),
                           wide_a[:, s, :].rearrange("p (g e) -> p g e", g=16),
                           bc(rden[:, s, :], 2, ROW), ALU.mult).then_inc(sg(f"{n}_qkn"), 1)
                    for s in TS:
                        tile(f"{n}_qkt", s)
                        v.tensor_copy(wide_a[:, s, BANK:2 * BANK], ps(s, BANK, BANK)).then_inc(sg(f"{n}_kts"), 1)

                    def add_causal(s):
                        for h2 in range(2):
                            tt(grouped(s, 8, ROW)[:, 4 * h2:4 * h2 + 4],
                               ps(s, h2 * BANK, 256).rearrange("p (g k) -> p g k", g=4),
                               bc(causal[:], 1, 4), ALU.add)

                    softmax_less_max(n, lambda s: grouped(s, 8, ROW), 8, add_causal)
                    for s in TS:
                        tile(f"{n}_exp", s)
                        v.tensor_reduce(den[:, s, 0:8], grouped(s, 8, ROW), AX.X, ALU.add)
                    v.drain()
                    v.reciprocal(rden[:, :, 0:8], den[:, :, 0:8])
                    v.drain()
                    for s in TS:
                        tile(f"{n}_pv", s)
                        o = wide_b[:, s, 0:BANK].rearrange("p (j k e) -> p j k e", j=4, k=2)
                        for k in range(2):
                            i = tt(o[:, :, k, :], ps(s, k * BANK, 256).rearrange("p (j e) -> p j e", j=4),
                                   bc(rden[:, s, 0:8].rearrange("p (j k) -> p j k", k=2)[:, :, k], 2, ROW),
                                   ALU.mult)
                        i.then_inc(sg(f"{n}_o"), 1)
                    for s in TS:
                        tile(f"{n}_wo", s)
                        tt(y[:, s, :], ps(s, BANK, D), y[:, s, :], ALU.add).then_inc(sg(f"{n}_y1"), 1)
                    v.drain()
                    for s in TS:
                        v.tensor_copy(h[:, s, 0:64], y[:, s, 0:64])
                    v.drain()
                    tiles(f"{n}_h2")
                    statistics(n, h)
                    tiles(f"{n}_rstd")
                    normalise(n, h, h)
                    for s in TS:
                        tile(f"{n}_gelu", s)
                        for c in range(FFC):
                            i = stt(wide_a[:, s, c * P:c * P + P], ps(s, c * P, P), b_1[:, L, 0, c:c + 1],
                                    wide_b[:, s, c * P:c * P + P], ALU.add, ALU.mult)
                        i.then_inc(sg(f"{n}_gated"), 1)
                    for s in TS:
                        tile(f"{n}_out", s)
                        tile(f"{n}_yb", s)
                        tt(y[:, s, :], ps(s, BANK, D), y[:, s, :], ALU.add).then_inc(sg(f"{n}_x"), 1)
                v.drain()
                for s in TS:
                    stt(x[:, s, :], y[:, s, :], gate[:, 4:5], x[:, s, :], ALU.mult, ALU.add)

                v.drain()
                statistics("l1a", x)
                tiles("l1a_rstd")
                tt(small[:], mv[:, :, 1], rstd[:], ALU.mult)
                v.drain()
                tt(small[:], small[:], rstd[:], ALU.mult)
                v.drain()
                ts(small[:], small[:], LN_EPS, None, ALU.add).then_inc(sg("l1a_ms"), G)
                for s in TS:
                    dve.wait_ge(sg(f"plug_in{s}"), it * 32 + 32)
                    ts(decay[:, s, :], plug[:, s, :], patch_row[:, 0:1], 0.0, ALU.subtract, ALU.max
                       ).then_inc(sg("l1a_decay"), 1)
                    ts(reach[:, s, :], plug[:, s, :], patch_row[:, 0:1], PATCH_B, ALU.is_ge, ALU.mult)
                tiles("l1a_rms")
                tt(small[:], rstd[:], small2[:], ALU.mult)
                v.drain()
                normalise("l1a", y, x, small)
                for s in TS:
                    tile("l1a_power", s)
                    for b in range(2):
                        r = slice(64 * b, 64 * b + 64)
                        i = tt(pick[r, s, b, :], decay[r, s, :], reach[r, s, :], ALU.mult)
                    i.then_inc(sg("l1a_pick"), 1)
                update("l1a", 1, BANK, "l1a_xb")

                layer_norm("l1f")
                for s in TS:
                    tile("l1f_lg", s)
                    v.tensor_copy(logits[:, s, :], ps(s, 0, E))
                v.drain()
                tt(rank_a[:], bc(logits[:], 2, E), bc(logits[:], 3, E), ALU.is_gt)
                tt(rank_b[:], bc(logits[:], 2, E), bc(logits[:], 3, E), ALU.is_equal)
                v.tensor_reduce(small[:], logits[:], AX.X, ALU.max)
                v.drain()
                for s in TS:
                    tt(rank_b[:, s], rank_b[:, s], before[:], ALU.mult)
                tt(logits[:], logits[:], bc(small[:], 2, E), ALU.subtract)
                v.drain()
                tt(rank_a[:], rank_a[:], rank_b[:], ALU.add)
                v.drain().then_inc(sg("l1f_less"), G)
                v.tensor_reduce(rank[:], rank_a[:], AX.X, ALU.add)
                v.drain()
                tiles("l1f_exp")
                stt(rank[:], rank[:], 2.0, rank_b[:, :, 0, :], ALU.is_lt, ALU.mult)
                v.drain()
                v.tensor_reduce(small[:], rank[:], AX.X, ALU.add)
                v.drain()
                v.reciprocal(small[:], small[:])
                v.drain()
                tt(rank[:], rank[:], bc(small[:], 2, E), ALU.mult)
                v.drain()
                for s in TS:
                    tt(vtmp[:, s, :].rearrange("p (e r) -> p e r", e=E),
                       ps(s, BANK, P).rearrange("p (e r) -> p e r", e=E), bc(rank[:, s, :], 2, R), ALU.mult
                       ).then_inc(sg("l1f_hw"), 1)
                update("l1f", 5, BANK)

                layer_norm("l2a")
                tiles("l2a_neg")
                softmax_less_max("l2a", lambda s: grouped(s, 8, ROW), 8, add_neg(neg2))
                divide_heads("l2a", vtmp)
                v.drain()
                for s in TS:
                    stt(x[:, s, :], vtmp[:, s, :], gate[:, 2:3], x[:, s, :], ALU.mult, ALU.add)

                def quantise(n, of, width, step, col, wait=None):
                    for s in TS:
                        if wait:
                            tile(wait, s)
                        v.tensor_reduce(small[:, s:s + 1], of(s), AX.X, ALU.max, apply_absolute_value=True)
                    v.drain()
                    ts(small[:], small[:], LN_EPS, None, ALU.max)
                    v.drain()
                    v.reciprocal(small2[:], small[:])
                    ts(small[:], small[:], tern_127[:, step:step + 1], None, ALU.mult)
                    v.drain()
                    ts(small2[:], small2[:], 127.0, None, ALU.mult)
                    if col is not None:
                        ts(small[:], small[:], gate[:, col:col + 1], None, ALU.mult)
                    v.drain()
                    for s in TS:
                        ts(wide_c[:, s, 0:width], of(s), small2[:, s:s + 1], 127.0, ALU.mult, ALU.min)
                    v.drain()
                    for s in TS:
                        ts(quant[:, s, 0:width], wide_c[:, s, 0:width], ROUND, -ROUND, ALU.add, ALU.add
                           ).then_inc(sg(f"{n}_q"), 1)

                def update_scaled(n, bias_done=None):
                    for s in TS:
                        tile(f"{n}_out", s)
                        if bias_done:
                            tile(bias_done, s)
                        stt(x[:, s, :], ps(s, BANK, D), small[:, s:s + 1], x[:, s, :], ALU.mult, ALU.add
                            ).then_inc(sg(f"{n}_x"), 1)

                layer_norm("l2f")
                v.drain()
                quantise("l2f", lambda s: y[:, s, :], D, 0, None)
                for s in TS:
                    tile("l2f_hid", s)
                    stt(wide_a[:, s, 0:HID], ps(s, BANK, HID), small[:, s:s + 1], b_t1[:], ALU.mult, ALU.add
                        ).then_inc(sg("l2f_pre"), 1)
                quantise("l2g", lambda s: wide_b[:, s, 0:HID], HID, 1, 6, "l2f_gelu")
                update_scaled("l2g", "l2f_xb")

                layer_norm("l3a")
                for s in TS:
                    tile("l3a_qkv", s)
                    for b in range(2):
                        i = v.tensor_copy(v16[64:128, s, b, :, 0:8],
                                          ps(s, BANK + b * D, D)[64:128].rearrange("p (h e) -> p h e", h=16))
                    i.then_inc(sg("l3a_v"), 1)
                for b in range(2):
                    n = f"l3a{b}"
                    softmax_less_max(n, lambda s: ps(s).rearrange("p (g k) -> p g k", g=8), 8)
                    for s in TS:
                        tile(f"{n}_pt", s)
                        v.tensor_copy(wide_c[:, s, BANK:2 * BANK], ps(s, BANK, BANK)).then_inc(sg(f"{n}_ptsb"), 1)

                    def part(s):
                        return ps(s, 0, 16 * 9)[64 * b:64 * b + 64].rearrange("p (h e) -> p h e", h=16)
                    for s in TS:
                        tile(f"{n}_pv", s)
                        v.reciprocal(rden[64 * b:64 * b + 64, s, :], part(s)[:, :, 8])
                    v.drain()
                    for s in TS:
                        tt(vtmp[64 * b:64 * b + 64, s, :].rearrange("p (h e) -> p h e", h=16),
                           part(s)[:, :, 0:8], bc(rden[64 * b:64 * b + 64, s, :], 2, 8), ALU.mult
                           ).then_inc(sg(f"{n}_o"), 1)
                update("l3a", 3, BANK, "l3a_xb")

                layer_norm("l3f")
                v.drain()
                quantise("l3f", lambda s: y[:, s, :], D, 2, None)
                for s in TS:
                    ts(vtmp[:, s, :], ident[:], small[:, s:s + 1], None, ALU.mult).then_inc(sg("l3f_diag"), 1)
                for s in TS:
                    tile("l3f_hid", s)
                    tile("l3f_sts", s)
                    tt(wide_a[:, s, 0:HID].rearrange("p (c t) -> p c t", c=4),
                       ps(s, 0, HID).rearrange("p (c t) -> p c t", c=4), bc(scale_t[:, s, :], 1, 4), ALU.mult)
                v.drain()

                def chan(buf, s, c):
                    return buf[:, s, c * P:c * P + P].rearrange("p (b t) -> p b t", b=2)
                for s in TS:
                    for c in range(4):
                        ts(chan(wide_b, s, c), chan(wide_a, s, c), conv_w[:, c, 1:2], conv_b[:, c:c + 1],
                           ALU.mult, ALU.add)
                v.drain()
                for s in TS:
                    for c in range(4):
                        to = chan(wide_b, s, c)[:, :, 1:ROW]
                        stt(to, chan(wide_a, s, c)[:, :, 0:ROW - 1], conv_w[:, c, 0:1], to, ALU.mult, ALU.add)
                v.drain()
                for s in TS:
                    for c in range(4):
                        to = chan(wide_b, s, c)[:, :, 0:ROW - 1]
                        i = stt(to, chan(wide_a, s, c)[:, :, 1:ROW], conv_w[:, c, 2:3], to, ALU.mult, ALU.add)
                    i.then_inc(sg("l3f_conv"), 1)
                quantise("l3g", lambda s: ps(s, 0, HID), HID, 3, 7, "l3f_act")
                for s in TS:
                    tile("l3g_out", s)
                    stt(x[:, s, :], ps(s, BANK, D), small[:, s:s + 1], x[:, s, :], ALU.mult, ALU.add
                        ).then_inc(sg("l3f_x"), 1)

        @block.tensor
        def _(pe):
            mm = nc.tensor.matmul

            pe.wait_ge(sg("consts"), 1)
            pe.wait_ge(sg("lens_f"), 1)
            mm(ps(0, 0, ROW)[0:B], lens[:], tri[:], start=True, stop=True).then_inc(sg("cum"), 1)
            pe.wait_ge(sg("bound"), 1)
            mm(ps(0, 0, B)[0:ROW], bound[:], ident[0:B, 0:B], start=True, stop=True).then_inc(sg("bound_tp"), 1)
            pe.wait_ge(sg("bound_ts"), 1)
            mm(ps(0, 0, ROW)[0:B], bound_t[:], tri[:], start=True, stop=True).then_inc(sg("plug_p"), 1)
            pe.wait_ge(sg("tern_rows"), 1)
            mm(ps(0, 0, 4), ones[:], tern_sum[:], start=True, stop=True).then_inc(sg("tern_all"), 1)
            pe.wait_ge(sg("setup_dve"), 1)

            with pe.Fori(0, PASSES) as it:

                def tile(name, s):
                    pe.wait_ge(sg(name), reached(name, it, s + 1))

                def turn_over(wait, done, of, at=0):
                    for s in TS:
                        tile(wait, s)
                        nc.tensor.transpose(ps(s, at, P), of(s), ident[:]).then_inc(sg(done), 1)

                def turn_many(wait, done, of, n, at):
                    for s in TS:
                        tile(wait, s)
                        for c in range(n):
                            i = nc.tensor.transpose(ps(s, at + c * P, P), of(s)[:, c * P:c * P + P], ident[:])
                        i.then_inc(sg(done), 1)

                def scores8(n, keys, waits):
                    for s in TS:
                        for w in waits:
                            tile(w, s)
                        for b in range(2):
                            for h4 in range(4):
                                i = mm(ps(s, h4 * P + b * ROW, ROW),
                                       wide_a[:, s, b * BANK + h4 * P:b * BANK + h4 * P + P],
                                       keys(s)[:, 64 * b:64 * b + 64], start=True, stop=True)
                        i.then_inc(sg(f"{n}_sc"), 1)

                def values8(n):
                    for s in TS:
                        tile(f"{n}_pts", s)
                        tile(f"{n}_v", s)
                        settle(pe, "pe_waits")
                        for hh in range(8):
                            for b in range(2):
                                r = slice(64 * b, 64 * b + 64)
                                i = mm(ps_all[r, s, b * BANK + hh * 17:b * BANK + hh * 17 + 17],
                                       wide_c[r, s, hh * ROW:hh * ROW + ROW], v8[r, s, hh, :],
                                       start=True, stop=True)
                        i.then_inc(sg(f"{n}_pv"), 1)

                turn_over("l0a_y", "l0a_yt", lambda s: y[:, s, :])
                for s in TS:
                    pe.wait_ge(sg(f"tile_in{s}"), (it + 1) * TILE_LOADS)
                    for c in range(2):
                        mm(ps(s, BANK, D), ctx_t[:, s, c, :], w_src[:, c, D:2 * D], start=(c == 0), stop=(c == 1))
                    tile("l0a_ht", s)
                    mm(ps(s, 0, P), w_tgt[:], ht[:, s, :], start=True, stop=True)
                    for c in range(2):
                        i = mm(ps(s, P, P), w_src[:, c, 0:D], ctx_t[:, s, c, :], start=(c == 0), stop=(c == 1))
                    i.then_inc(sg("l0a_qkv"), 1)
                scores8("l0a", lambda s: kt[:, s, :], ("l0a_spread", "l0a_v"))
                turn_many("l0a_exp", "l0a_pt", lambda s: wide_b[:, s, 0:BANK], 4, BANK)
                values8("l0a")
                turn_over("l0a_o", "l0a_ot", lambda s: vtmp[:, s, :])
                for s in TS:
                    tile("l0a_ots", s)
                    mm(ps(s, BANK, D), ht[:, s, :], w_out[:, 0, :], start=True, stop=False)
                    mm(ps(s, BANK, D), qt[:, s, :], w_out[:, 1, :], start=False, stop=True).then_inc(
                        sg("l0a_out"), 1)

                for L in range(2):
                    n = f"l0f{L}"
                    turn_over("l0f_y" if L == 0 else "l0f0_x", f"{n}_yt", lambda s: y[:, s, :])
                    for s in TS:
                        tile(f"{n}_hs", s)
                        hs = ht_shift[:, s, :, :].rearrange("p b t -> p (b t)")
                        for q in range(2):
                            i = mm(ps(s, q * BANK, BANK), hs, w_qkv[:, L, q * INNER:q * INNER + INNER],
                                   start=True, stop=True)
                        i.then_inc(sg(f"{n}_qk"), 1)
                    for s in TS:
                        tile(f"{n}_turned", s)
                        for b in range(2):
                            for half in range(2):
                                i = mm(ps_all[64 * half:64 * half + 64, s, b * BANK:b * BANK + BANK],
                                       ht_shift[:, s, b, :], w_qkv[:, L, 2 * INNER:3 * INNER],
                                       start=True, stop=True)
                        i.then_inc(sg(f"{n}_v"), 1)
                    for s in TS:
                        tile(f"{n}_qkn", s)
                        tile(f"{n}_vs", s)
                        for c in range(8):
                            i = nc.tensor.transpose(ps(s, c * P, P), wide_b[:, s, c * P:c * P + P], ident[:])
                        i.then_inc(sg(f"{n}_qkt"), 1)
                    for s in TS:
                        tile(f"{n}_qts", s)
                        tile(f"{n}_kts", s)
                        settle(pe, "pe_waits")
                        for c in range(4):
                            for b in range(2):
                                for h2 in range(2):
                                    r = slice(64 * h2, 64 * h2 + 64)
                                    col = c * P + 64 * b
                                    i = mm(ps_all[64 * b:64 * b + 64, s, h2 * BANK + c * ROW:h2 * BANK + c * ROW + ROW],
                                           wide_a[r, s, col:col + 64], wide_a[r, s, BANK + col:BANK + col + 64],
                                           start=True, stop=True)
                        i.then_inc(sg(f"{n}_sc"), 1)
                    turn_many(f"{n}_exp", f"{n}_pt", lambda s: wide_b[:, s, 0:BANK], 4, 0)
                    for s in TS:
                        tile(f"{n}_pts", s)
                        settle(pe, "pe_waits")
                        for j in range(4):
                            for b in range(2):
                                for k in range(2):
                                    head = 4 * (j % 2) + 2 * k + j // 2
                                    r = slice(64 * k, 64 * k + 64)
                                    i = mm(ps_all[64 * b:64 * b + 64, s, k * BANK + j * ROW:k * BANK + j * ROW + ROW],
                                           wide_a[r, s, j * P + 64 * b:j * P + 64 * b + 64],
                                           wide_c[r, s, b * BANK + head * ROW:b * BANK + head * ROW + ROW],
                                           start=True, stop=True)
                        i.then_inc(sg(f"{n}_pv"), 1)
                    turn_many(f"{n}_o", f"{n}_ot", lambda s: wide_b[:, s, 0:BANK], 4, 0)
                    for s in TS:
                        tile(f"{n}_ots", s)
                        for c in range(4):
                            i = mm(ps(s, BANK, D), wide_a[:, s, c * P:c * P + P], w_o[:, L, c, :],
                                   start=(c == 0), stop=(c == 3))
                        i.then_inc(sg(f"{n}_wo"), 1)
                    for s in TS:
                        tile(f"{n}_y1", s)
                        mm(ps(s, 0, 64), shift[:], y[:, s, 64:128], start=True, stop=True).then_inc(
                            sg(f"{n}_sh"), 1)
                    turn_over(f"{n}_y", f"{n}_lt", lambda s: h[:, s, :])
                    for s in TS:
                        tile(f"{n}_lts", s)
                        for half in range(2):
                            for c in range(FFC):
                                i = mm(ps(s, half * BANK + c * P, P), w_1[:, L, half, c, :], ht[:, s, :],
                                       start=True, stop=True)
                        i.then_inc(sg(f"{n}_hid"), 1)
                    for s in TS:
                        tile(f"{n}_gated", s)
                        for c in range(FFC):
                            i = mm(ps(s, BANK, D), wide_a[:, s, c * P:c * P + P], w_2[:, L, c, :],
                                   start=(c == 0), stop=(c == FFC - 1))
                        i.then_inc(sg(f"{n}_out"), 1)

                turn_over("l1a_y", "l1a_yt", lambda s: y[:, s, :])
                for s in TS:
                    tile("l1a_ht", s)
                    tile("l1a_pick", s)
                    mm(ps(s, BANK, D), ht[:, s, :], w_in[:], start=True, stop=False)
                    mm(ps(s, BANK, D), pick[:, s, :, :].rearrange("p b t -> p (b t)"), patches[:, s, :],
                       start=False, stop=True).then_inc(sg("l1a_out"), 1)

                turn_over("l1f_y", "l1f_yt", lambda s: y[:, s, :])
                for s in TS:
                    tile("l1f_ht", s)
                    mm(ps(s, 0, E), ht[:, s, :], w_gate[:], start=True, stop=True)
                    mm(ps(s, BANK, P), ht[:, s, :], w_a[:], start=True, stop=True).then_inc(sg("l1f_lg"), 1)
                turn_over("l1f_hw", "l1f_hwt", lambda s: vtmp[:, s, :])
                for s in TS:
                    tile("l1f_hwts", s)
                    mm(ps(s, BANK, D), ht[:, s, :], w_b[:], start=True, stop=True).then_inc(sg("l1f_out"), 1)

                turn_over("l2a_y", "l2a_yt", lambda s: y[:, s, :])
                scores8("l2a", lambda s: ctx_t[:, s, 0, :], ("l2a_spread",))
                turn_many("l2a_exp", "l2a_pt", lambda s: wide_b[:, s, 0:BANK], 4, BANK)
                values8("l2a")

                def turn_quantised(n, k):
                    for s in TS:
                        tile(f"{n}_q", s)
                        for c in range(k):
                            i = nc.tensor.transpose(ps(s, c * P // 2, P // 2).bitcast(BF16),
                                                    quant[:, s, c * P:c * P + P], ident_bf[:])
                        i.then_inc(sg(f"{n}_qt"), 1)

                def down(n, w):
                    for s in TS:
                        tile(f"{n}_qts", s)
                        for c in range(4):
                            i = mm(ps(s, BANK, D), quant_t[:, s, c * P:c * P + P], tern[:, w, c * P:c * P + P],
                                   start=(c == 0), stop=(c == 3))
                        i.then_inc(sg(f"{n}_out"), 1)

                turn_quantised("l2f", 1)
                for s in TS:
                    tile("l2f_qts", s)
                    mm(ps(s, BANK, HID), quant_t[:, s, 0:P], tern[:, 0, :], start=True, stop=True).then_inc(
                        sg("l2f_hid"), 1)
                turn_quantised("l2g", 4)
                down("l2g", 1)

                turn_over("l3a_y", "l3a_yt", lambda s: y[:, s, :])
                for s in TS:
                    tile("l3a_ht", s)
                    for q in range(2):
                        mm(ps(s, q * P, P), w_qkv3[:, q * D:q * D + D], ht[:, s, :], start=True, stop=True)
                    for b in range(2):
                        i = mm(ps_all[64:128, s, BANK + b * D:BANK + b * D + D], ht[:, s, 64 * b:64 * b + 64],
                               w_qkv3[:, 2 * D:3 * D], start=True, stop=True)
                    i.then_inc(sg("l3a_qkv"), 1)
                for b in range(2):
                    n = f"l3a{b}"
                    for s in TS:
                        tile(f"{n}_spread", s)
                        if b == 0:
                            tile("l3a_v", s)
                            tile("l3_ctx", s)
                        else:
                            tile("l3a0_o", s)
                        for c in range(8):
                            i = mm(ps(s, c * P, P), wide_a[:, s, c * P:c * P + P],
                                   k_cat[:, s, b, :, :].rearrange("p a t -> p (a t)"), start=True, stop=True)
                        i.then_inc(sg(f"{n}_sc"), 1)
                    turn_many(f"{n}_exp", f"{n}_pt", lambda s: wide_b[:, s, :], 8, 0)
                    for s in TS:
                        tile(f"{n}_ptsa", s)
                        tile(f"{n}_ptsb", s)
                        for hh in range(16):
                            i = mm(ps_all[64 * b:64 * b + 64, s, hh * 9:hh * 9 + 9],
                                   wide_c[:, s, hh * ROW:hh * ROW + ROW], v16[:, s, b, hh, :],
                                   start=True, stop=True)
                        i.then_inc(sg(f"{n}_pv"), 1)
                for s in TS:
                    tile("l3a1_o", s)
                    nc.tensor.transpose(ps(s, 0, P), vtmp[:, s, :], ident[:]).then_inc(sg("l3a_ot"), 1)
                for s in TS:
                    tile("l3a_ots", s)
                    mm(ps(s, BANK, D), qt[:, s, :], w_proj3[:], start=True, stop=True).then_inc(sg("l3a_out"), 1)

                for s in TS:
                    tile("l3f_diag", s)
                    mm(ps(s, BANK, P), ones[:], vtmp[:, s, :], start=True, stop=True).then_inc(sg("l3f_st"), 1)
                turn_quantised("l3f", 1)
                for s in TS:
                    tile("l3f_qts", s)
                    for c in range(4):
                        i = mm(ps(s, c * P, P), tern[:, 2, c * P:c * P + P], quant_t[:, s, 0:P],
                               start=True, stop=True)
                    i.then_inc(sg("l3f_hid"), 1)
                turn_many("l3f_silu", "l3f_act", lambda s: wide_b[:, s, 0:BANK], 4, 0)
                turn_quantised("l3g", 4)
                down("l3g", 3)


def rotary_table(np):
    half = np.arange(0, ROW, 2, dtype=np.float32)
    freq = np.arange(ROW, dtype=np.float32)[:, None] * (1.0 / 10000.0 ** (half / ROW))[None]
    freq = np.concatenate([freq, freq], -1)
    base = (half + 0.4 * ROW) / (1.4 * ROW)
    scale = base[None] ** ((np.arange(ROW, dtype=np.float32) - ROW // 2) / 32.0)[:, None]
    scale = np.concatenate([scale, scale], -1)
    sign = np.where(np.arange(ROW) < ROW // 2, -1.0, 1.0)[None]
    cos, sin = np.cos(freq), np.sin(freq) * sign
    t = np.stack([np.stack([8 * cos * scale, 8 * sin * scale], 1), np.stack([cos / scale, sin / scale], 1)], 1)
    return np.concatenate([t, t], 0).astype(np.float32)


def laid_out(i):
    import numpy as np

    def rep(a, n=P):
        return np.broadcast_to(a[None], (n,) + a.shape)

    def col(a):
        return a.reshape(-1, 1)

    def heads(w):
        w = w.reshape(2, 8, ROW, D)
        order = [4 * (j % 2) + 2 * k + j // 2 for j in range(4) for k in range(2)]
        return w[:, order].reshape(2, 4, P, D).transpose(2, 0, 1, 3)

    def chunked(a, axis):
        pad = [(0, 0)] * a.ndim
        pad[axis] = (0, FFC * P - FF)
        return np.pad(a, pad)

    w1 = i["L0_ffn_w1"].reshape(2, D, 2, FF)
    b1 = i["L0_ffn_b1"].reshape(2, 2, FF)
    ctx = i["ctx_2048"].reshape(PASSES, G, P, CTX)
    row = np.ascontiguousarray
    wide = lambda w: w.T.reshape(4, P, D).transpose(1, 0, 2).reshape(P, HID)
    a = {
        "x": i["x"].reshape(PASSES, G, P, D),
        "ctx": ctx,
        "ctx_t": ctx.reshape(PASSES, G, P, 2, P).transpose(0, 1, 4, 3, 2),
        "mask_f": i["mask_BxS2_fk1"].reshape(PASSES, G, P),
        "mask_i": i["mask_BxS2_ik0"].reshape(PASSES, G, P),
        "lens_t": i["mask_BxS2_if0"].T,
        "w_src": i["L0_xattn_W_src"].T.reshape(2, P, 2 * D).transpose(1, 0, 2),
        "w_tgt": i["L0_xattn_W_tgt"].T,
        "w_out": i["L0_xattn_W_out"].T.reshape(2, P, D).transpose(1, 0, 2),
        "b_q": col(i["L0_xattn_b_tgt"]), "b_k": col(i["L0_xattn_b_src"][:D]), "b_v": rep(i["L0_xattn_b_src"][D:]),
        "w_qkv": i["L0_ffn_wqkv"].transpose(1, 0, 2), "w_o": heads(i["L0_ffn_wo"]),
        "w_1": chunked(w1, 3).reshape(2, D, 2, FFC, P).transpose(1, 0, 2, 3, 4),
        "w_2": chunked(i["L0_ffn_w2"], 1).reshape(2, FFC, P, D).transpose(2, 0, 1, 3),
        "b_1": chunked(b1, 2).reshape(2, 2, FFC, P).transpose(3, 0, 1, 2),
        "b_2": rep(i["L0_ffn_b2"]), "ln_g": i["L0_ffn_ln_g"].T, "ln_b": i["L0_ffn_ln_b"].T,
        "qk_scale": rep(np.stack([i["L0_ffn_q_scale"], i["L0_ffn_k_scale"]], 1)),
        "rotary": rotary_table(np),
        "w_in": i["L1_xattn_W_in"].T, "g_res": col(i["L1_xattn_g_res"]), "g_init": rep(i["L1_xattn_g_init"][:D]),
        "w_gate": i["L1_ffn_Wg"], "w_a": i["L1_ffn_A"].transpose(1, 0, 2).reshape(D, E * R),
        "w_b": i["L1_ffn_B"].reshape(E * R, D), "logit_b": rep(i["L2_xattn_b"]),
        "tern": np.stack([i["L2_ffn_W1"].T, wide(i["L2_ffn_W2"]), i["L3_ffn_w1"].T, wide(i["L3_ffn_w2"])], 1),
        "b_t1": rep(i["L2_ffn_b1"]),
        "w_qkv3": i["L3_xattn_w_qkv"].T, "w_proj3": i["L3_xattn_w_proj"].T,
        "conv_w": i["L3_ffn_conv_w"].reshape(4, P, 3).transpose(1, 0, 2),
        "conv_b": i["L3_ffn_conv_b"].reshape(4, P).T,
        "gate_in": rep(np.concatenate([i["g_xattn"], i["g_ffn"]])),
        "bias_in": rep(np.stack([i["L0_xattn_b_out"], i["L1_xattn_b_in"], i["L2_ffn_b2"], i["L3_xattn_b_proj"]])),
    }
    return {k: row(v) for k, v in a.items()}


def kernel(**inputs):
    import numpy as np
    import concourse.bacc as bacc
    from concourse.bass_utils import run_bass_kernel_spmd

    nc = bacc.Bacc("TRN2", target_bir_lowering=False, num_devices=1)
    arrays, d = {}, {}
    for name, a in laid_out({k: np.asarray(v) for k, v in inputs.items()}).items():
        arrays[f"in_{name}"] = a
        d[name] = nc.dram_tensor(f"in_{name}", a.shape, mybir.dt.from_np(a.dtype), kind="ExternalInput").ap()
    out = nc.dram_tensor("out", (PASSES, G, P, D), F32, kind="ExternalOutput").ap()
    flamingo_stack(nc, d, out)
    r = run_bass_kernel_spmd(nc, [arrays], core_ids=[0])
    return r.results[0]["out"].reshape(B, ROW, D)
```

```python
from contextlib import ExitStack
import math

import concourse.bass as bass
from concourse import mybir

ALU = mybir.AluOpType
ACT = mybir.ActivationFunctionType
AX = mybir.AxisListType
F32 = mybir.dt.float32
BF16 = mybir.dt.bfloat16
I32 = mybir.dt.int32

P = 128
D = 128
ROW = 64
B = 64
G = 4
TILES = B * ROW // P
PASSES = TILES // G
CTX = 256
HID = 512
INNER = 512
FF, FFC = 341, 3
E, R = 8, 16
LN_EPS = 1e-5
NEG = -1e30
ROUND = 1.5 * 2.0 ** 23
PATCH_EPS = 1e-3
PATCH_DT = -math.log(-math.expm1(-PATCH_EPS))
PATCH_B = math.exp(-PATCH_EPS)
BANK = 512

PARTS = tuple(
    {name: int(at) for name, at in (stage.split() for stage in text.split(","))}
    for text in (
        """
        l0a_neg 0, patch_sq 1, l0a_var 3, patch_var 4, l0a_rstd 5, patch_rstd 7, l0a_y 8, l0a_xb 44, l0a_yt
        25, l0a_ht 29, l0a_qkv 45, l0a_qk 49, l0a_v 49, patches 53, l0a_spread 54, l0a_sc 65, l0a_max 70,
        l0a_sub 73, l0a_exp 77, l0a_pt 80, l0a_pts 85, l0a_pv 94, l0a_o 101, l0a_ot 115, l0a_ots 116,
        l0a_out 119, l0a_x 124, l0f_var 126, l0f_rstd 128, l0f_y 132, l0f0_yt 133, l0f0_hs 138, l0f0_qk 145,
        l0f0_sq 148, l0f0_turned 152, l0f0_v 165, l0f0_vs 175, l0f0n_var 160, l0f0n_rstd 162, l0f0_rot 171,
        l0f0_qkn 178, l0f0_qkt 187, l0f0_qts 190, l0f0_sc 199, l0f0_max 208, l0f0_sub 213, l0f0_exp 216
        """,
        """
        l0f0_pt 15, l0f0_pts 11, l0f0_pv 18, l0f0_o 30, l0f0_ot 39, l0f0_ots 47, l0f0_wo 51, l0f0_y1 56,
        l0f0_sh 60, l0f0_h2 59, l0f0_var 63, l0f0_rstd 66, l0f0_y 72, l0f0_yb 76, l0f0_lt 79, l0f0_lts 82,
        l0f0_hid 86, l0f0_bent 93, l0f0_gated 96, l0f0_out 102, l0f0_x 104, l0f1_yt 113, l0f1_hs 118,
        l0f1_qk 120, l0f1_sq 131, l0f1_turned 135, l0f1_v 149, l0f1_vs 158, l0f1n_var 142, l0f1n_rstd 144,
        l0f1_rot 153, l0f1_qkn 164, l0f1_qkt 174, l0f1_qts 185, l0f1_sc 189, l0f1_max 194, l0f1_sub 198,
        l0f1_exp 203
        """,
        """
        l0f1_pt 17, l0f1_pts 10, l0f1_pv 17, l0f1_o 19, l0f1_ot 21, l0f1_ots 24, l0f1_wo 28, l0f1_y1 32,
        l0f1_sh 34, l0f1_h2 37, l0f1_var 35, l0f1_rstd 38, l0f1_y 40, l0f1_yb 42, l0f1_lt 43, l0f1_lts 46,
        l0f1_hid 48, l0f1_bent 52, l0f1_gated 57, l0f1_out 62, l0f1_x 64, l2a_neg 67, l1a_var 68, l1a_rstd
        71, l1am_var 74, l1a_decay 75, l1a_power 87, l1am_rstd 78, l1a_y 81, l1a_pick 89, l1a_xb 83, l1a_yt
        84, l1a_ht 88, l1a_out 92, l1a_x 91, l1f_var 95, l1f_rstd 97, l1f_y 99, l1f_yt 100, l1f_ht 103,
        l1f_lg 105, l1f_less 108, l1f_exp 110, l1f_o 109, l1f_ot 111, l1f_ots 114, l1f_out 117, l1f_x 121,
        l2a_v 106, l2a_var 123, l2a_rstd 125, l2a_y 127, l2a_yt 129, l2a_ht 134, l2a_spread 137, l3_ctx 140,
        l2a_sc 141, l2a_max 146, l2a_sub 150, l2a_exp 154, l2a_pt 156, l2a_pts 157, l2a_pv 159, l2a_o 166,
        l3_ctx_used 167, l2f_var 170, l2f_rstd 177, l2f_y 181, l2f_xb 202, l2f_q 183, l2f_qt 191, l2f_qts
        192, l2f_hid 193, l2f_pre 197, l2f_bent 201, l2g_rounded 204, l2g_q 209, l2g_qt 211, l2g_qts 214,
        l2g_out 215, l2g_x 212
        """,
        """
        l3a_var 9, l3a_rstd 12, l3a_y 14, l3a_xb 16, l3a_yt 20, l3a_ht 22, l3a_qkv 23, l3a_qk 27, l3a_v 26,
        l3a0_spread 31, l3a0_sc 36, l3a0_sub 41, l3a0_exp 50, l3a0_pt 55, l3a0_pts 61, l3a0_pv 69, l3a0_o
        90, l3a1_spread 98, l3a1_sc 107, l3a1_sub 112, l3a1_exp 122, l3a1_pt 130, l3a1_pts 136, l3a1_pv 139,
        l3a1_o 143, l3a_ot 147, l3a_ots 151, l3a_out 155, l3a_x 161, l3f_var 163, l3f_rstd 169, l3f_y 172,
        l3f_q 173, l3f_diag 176, l3f_st 179, l3f_qt 180, l3f_qts 182, l3f_sts 184, l3f_hid 186, l3f_conv
        188, l3f_bent 195, l3f_act 196, l3g_rounded 200, l3g_q 205, l3g_qt 206, l3g_qts 207, l3g_out 210,
        l3f_x 217
        """,
    )
)

KINDS = {
    "transposed": ("yt", "pt", "ot", "qkt", "lt", "qt", "act"),
    "multiplied": ("qkv", "l0f0_qk", "l0f1_qk", "l0f0_v", "l0f1_v", "out", "wo", "hid", "lg", "st", "sh"),
    "scored": ("sc",),
    "weighted": ("pv",),
    "moved": ("ht", "hs", "pts", "ots", "qts", "vs", "h2", "lts", "l3a_qk", "sts"),
    "activated": ("exp", "power", "bent", "l0f0_sq", "l0f1_sq", "patch_sq"),
    "measured": ("var",),
    "normalised": ("y",),
    "less_max": ("l3a0_sub", "l3a1_sub"),
    "maxima": ("max",),
    "rounded": ("rounded",),
    "divided": ("o",),
    "updated": ("x", "y1"),
    "rotated": ("turned", "qkn"),
    "prepared": ("l0a_qk", "l0a_v", "l3a_v", "patches", "pick", "decay"),
    "quantised": ("l2f_q", "l3f_q", "diag"),
    "unrounded": ("l2g_q", "l3g_q"),
    "shaped": ("gated", "pre", "conv", "less"),
    "inverse_roots": ("rstd",),
    "biased": ("xb", "yb"),
    "spread": ("spread",),
    "centred": ("l0a_sub", "l0f0_sub", "l0f1_sub", "l2a_sub"),
    "summed": ("rot",),
    "masks": ("neg",),
    "context": ("l2a_v", "l3_ctx"),
    "context_used": ("l3_ctx_used",),
}


def kind_of(name):
    role = name.rpartition("_")[2]
    for kind, names in KINDS.items():
        if name in names:
            return kind
    return next(kind for kind, names in KINDS.items() if role in names)


PLACES = {}
for _part in PARTS:
    for _name in _part:
        PLACES[_name] = (kind_of(_name), sum(kind == kind_of(_name) for kind, _ in PLACES.values()))
STAGES_OF = {kind: sum(k == kind for k, _ in PLACES.values()) for kind in KINDS}


def side_by_side(*chains):
    at = [[part, stages, next(stages, None)] for part, stages in chains]
    while any(name for _, _, name in at):
        entry = min(at, key=lambda e: PARTS[e[0]][e[2]] if e[2] else math.inf)
        entry[2] = next(entry[1], None)


def all_passes(eng, part):
    last = PASSES - 1
    for n in range(3):
        side_by_side(*((n - s, part(n - s, s, 0, 0)) for s in range(n + 1)))
    with eng.Fori(0, PASSES - 1) as it:
        for n in range(3, 7):
            side_by_side(*(((n - s) % 4, part((n - s) % 4, s, it, (n - s) // 4)) for s in range(G)))
    side_by_side(*((3 - s, part(3 - s, s, last, 0)) for s in range(G)))
    for n in range(4, 7):
        side_by_side(*((n - s, part(n - s, s, last, 0)) for s in range(n - 3, G)))


def flamingo_stack(nc, d, out):
    ctx = ExitStack()
    with ctx:
        def sb(name, shape, dt=F32):
            return ctx.enter_context(nc.sbuf_tensor(name, shape, dt))

        semaphores = {}

        def signal(name, s=None):
            name = name if s is None else f"{PLACES[name][0]}_{s}"
            if name not in semaphores:
                semaphores[name] = ctx.enter_context(nc.semaphore(name))
            return semaphores[name]

        def reached(name, it, ahead=0):
            kind, at = PLACES[name]
            return it * STAGES_OF[kind] + (ahead * STAGES_OF[kind] + at + 1)

        def bc(ap, axis, n):
            shape = list(ap.shape)
            return ap.unsqueeze(axis).to_broadcast(shape[:axis] + [n] + shape[axis:])

        ident = sb("ident", [P, P])
        ident_bf = sb("ident_bf", [P, P], BF16)
        ones = sb("ones", [P, P])
        shift = sb("shift", [P, P])
        causal = sb("causal", [P, ROW])
        tri = sb("tri", [ROW, ROW])
        before = sb("before", [P, E, E])
        head8 = sb("head8", [P, 8])
        head16 = sb("head16", [P, 16])
        minus_half = sb("minus_half", [P, 64])
        ln_eps = sb("ln_eps", [P, 1])
        minus_round = sb("minus_round", [P, 1])
        patch_row = sb("patch_row", [P, 1])
        position = sb("position", [ROW, ROW])
        w_src = sb("w_src", [P, 2, 2 * D])
        w_tgt = sb("w_tgt", [P, D])
        w_out = sb("w_out", [P, 2, D])
        b_q = sb("b_q", [P, 1])
        b_k = sb("b_k", [P, 1])
        b_v = sb("b_v", [P, D])
        w_qkv = sb("w_qkv", [P, 2, 3 * INNER])
        w_o = sb("w_o", [P, 2, 4, D])
        w_1 = sb("w_1", [P, 2, 2, FFC, P])
        w_2 = sb("w_2", [P, 2, FFC, D])
        b_1 = sb("b_1", [P, 2, 2, FFC])
        b_2 = sb("b_2", [P, 2, D])
        ln_g = sb("ln_g", [P, 2])
        ln_b = sb("ln_b", [P, 2])
        qk_scale = sb("qk_scale", [P, 2, 2, ROW])
        rotary = sb("rotary", [P, 2, 2, ROW])
        turn = sb("turn", [P, 2, 2, 2, ROW])
        w_in = sb("w_in", [P, D])
        g_res = sb("g_res", [P, 1])
        g_init = sb("g_init", [P, D])
        w_gate = sb("w_gate", [P, E])
        w_a = sb("w_a", [P, E * R])
        w_b = sb("w_b", [P, D])
        logit_b = sb("logit_b", [P, 1])
        raw = sb("raw", [P, 4, HID])
        tern = sb("tern", [P, 4, HID], BF16)
        tern_sum = sb("tern_sum", [P, 4])
        tern_step = sb("tern_step", [P, 4])
        tern_inv = sb("tern_inv", [P, 4])
        tern_127 = sb("tern_127", [P, 4])
        b_t1 = sb("b_t1", [P, HID])
        w_qkv3 = sb("w_qkv3", [P, 3 * D])
        w_proj3 = sb("w_proj3", [P, D])
        conv_w = sb("conv_w", [P, 4, 3])
        conv_b = sb("conv_b", [P, 4])
        gate_in = sb("gate_in", [P, 8])
        gate = sb("gate", [P, 8])
        bias_in = sb("bias_in", [P, 4, D])
        bias = sb("bias", [P, 4, D])
        lens_i = sb("lens_i", [ROW, B], I32)
        lens = sb("lens", [ROW, B])
        last = sb("last", [B, ROW])
        wrap = sb("wrap", [B, ROW])
        bound = sb("bound", [B, ROW])
        bound_t = sb("bound_t", [ROW, B])
        plug_all = sb("plug_all", [B, ROW])

        xin = sb("xin", [P, G, D])
        x = sb("x", [P, G, D])
        ctx_s = sb("ctx_s", [P, G, CTX])
        ctx_t = sb("ctx_t", [P, G, 2, P])
        ctx_v = sb("ctx_v", [ROW, G, 2, D])
        mask_row = sb("mask_row", [P, G, P])
        mask_col = sb("mask_col", [P, G, 1])
        mask_i = sb("mask_i", [P, G, P], I32)
        plug = sb("plug", [P, G, ROW])
        neg0 = sb("neg0", [P, G, P])
        neg2 = sb("neg2", [P, G, P])
        stats = sb("stats", [P, G, 6])
        mv = sb("mv", [P, G, 2])
        var_eps = sb("var_eps", [P, G])
        rstd = sb("rstd", [P, G])
        small = sb("small", [P, G])
        small2 = sb("small2", [P, G])
        ctx_sq = sb("ctx_sq", [P, G])
        y = sb("y", [P, G, D])
        h_in = sb("h_in", [P, G, D])
        vtmp = sb("vtmp", [P, G, D])
        ht = sb("ht", [P, G, P])
        ht_shift = sb("ht_shift", [P, G, 2, ROW])
        qt = sb("qt", [P, G, P])
        kt = sb("kt", [P, G, P])
        k_cat = sb("k_cat", [P, G, 2, 2, ROW])
        v8 = sb("v8", [P, G, 8, 17])
        v16 = sb("v16", [P, G, 2, 16, 9])
        patches = sb("patches", [P, G, D])
        pick = sb("pick", [P, G, 2, ROW])
        decay = sb("decay", [P, G, ROW])
        reach = sb("reach", [P, G, ROW])
        mx = sb("mx", [P, G, 16])
        den = sb("den", [P, G, 16])
        rden = sb("rden", [P, G, 16])
        wide_a = sb("wide_a", [P, G, 2 * BANK])
        wide_b = sb("wide_b", [P, G, 2 * BANK])
        wide_c = sb("wide_c", [P, G, 2 * BANK])
        quant = sb("quant", [P, G, HID], BF16)
        quant_t = sb("quant_t", [P, G, HID], BF16)
        scale_t = sb("scale_t", [P, G, P])
        logits = sb("logits", [P, G, E])
        rank_a = sb("rank_a", [P, G, E, E])
        rank_b = sb("rank_b", [P, G, E, E])
        rank = sb("rank", [P, G, E])

        ps_all = ctx.enter_context(nc.psum_tensor("ps_all", [P, G, 2 * BANK], F32))
        plug_dram = nc.dram_tensor("plug_dram", [B, ROW], F32, kind="Internal").ap()

        def ps(s, a=0, n=2 * BANK):
            return ps_all[:, s, a:a + n]

        TILE_IN = ("xin", "ctx_s", "ctx_t", "ctx_v", "mask_row", "mask_i")
        TILE_LOADS = 16 * len(TILE_IN)

        once = [
            (w_src, d["w_src"]), (w_tgt, d["w_tgt"]), (w_out, d["w_out"]), (b_q, d["b_q"]), (b_k, d["b_k"]),
            (b_v, d["b_v"]), (w_qkv, d["w_qkv"]), (w_o, d["w_o"]), (b_2, d["b_2"]), (ln_g, d["ln_g"]),
            (ln_b, d["ln_b"]), (qk_scale, d["qk_scale"]), (rotary, d["rotary"]), (w_in, d["w_in"]),
            (g_res, d["g_res"]), (g_init, d["g_init"]), (w_gate, d["w_gate"]), (w_a, d["w_a"]), (w_b, d["w_b"]),
            (logit_b, d["logit_b"]), (raw, d["tern"]), (b_t1, d["b_t1"]), (w_qkv3, d["w_qkv3"]),
            (w_proj3, d["w_proj3"]), (conv_w, d["conv_w"]), (conv_b, d["conv_b"]), (gate_in, d["gate_in"]),
            (bias_in, d["bias_in"]), (w_1, d["w_1"]), (w_2, d["w_2"]), (b_1, d["b_1"]),
        ]

        def settle(eng, count):
            eng.sem_inc(signal(count), 1)

        def loaded(it, ahead, n):
            return it * n + (ahead + 1) * n

        nc.disable_value_cache = True
        block = ctx.enter_context(nc.Block())

        @block.sync
        def _(sp):
            def load(it, s, names):
                what = {
                    "xin": (xin[:, s, :], d["x"][it, s]),
                    "ctx_s": (ctx_s[:, s, :], d["ctx"][it, s]),
                    "ctx_t": (ctx_t[:, s, :, :], d["ctx_t"][it, s]),
                    "ctx_v": (ctx_v[:, s, :, :], d["ctx"][it, s, :, D:CTX].rearrange("(b t) f -> t b f", b=2)),
                    "mask_row": (mask_row[:, s, :], d["mask_f"][it, s].partition_broadcast(P)),
                    "mask_col": (mask_col[:, s, :], d["mask_f"][it, s].unsqueeze(1)),
                    "mask_i": (mask_i[:, s, :], d["mask_i"][it, s].partition_broadcast(P)),
                }
                for name in names:
                    to, of = what[name]
                    done = "mask_col_in" if name == "mask_col" else "tile_in"
                    sp.dma_start(to, of).then_inc(signal(f"{done}{s}"), 16)

            def load_plug(it, s):
                for b in range(2):
                    rows = plug_dram.rearrange("(i s b) l -> i s b l", s=G, b=2)[it, s, b]
                    sp.dma_start(plug[64 * b:64 * b + 64, s, :], rows.partition_broadcast(ROW)).then_inc(
                        signal(f"plug_in{s}"), 16)

            sp.dma_start(lens_i[:], d["lens_t"]).then_inc(signal("lens_in"), 16)
            for s in range(G):
                load(0, s, TILE_IN + ("mask_col",))
            for n, (to, of) in enumerate(once):
                sp.dma_start(to[:], of).then_inc(signal("weights_in"), 16)
            sp.wait_ge(signal("plug_made"), 1)
            sp.dma_start(plug_dram, plug_all[:]).then_inc(signal("plug_kept"), 16)
            sp.wait_ge(signal("plug_kept"), 16)
            for s in range(G):
                load_plug(0, s)
            with sp.Fori(0, PASSES - 1) as it:
                for s in range(G):
                    sp.wait_ge(signal("l3_ctx_used", s), reached("l3_ctx_used", it))
                    load(it + 1, s, TILE_IN)
                    load_plug(it + 1, s)
                    sp.wait_ge(signal("l3f_x", s), reached("l3f_x", it))
                    sp.dma_start(out[it, s], x[:, s, :]).then_inc(signal(f"stored{s}"), 16)
                    sp.wait_ge(signal(f"stored{s}"), it * 16 + 16)
                    load(it + 1, s, ("mask_col",))
            for s in range(G):
                sp.wait_ge(signal("l3f_x", s), reached("l3f_x", PASSES - 1))
                sp.dma_start(out[PASSES - 1, s], x[:, s, :]).then_inc(signal(f"stored{s}"), 16)
            for s in range(G):
                sp.wait_ge(signal(f"stored{s}"), 16 * PASSES)

        @block.gpsimd
        def _(pool):
            gp = nc.gpsimd

            def tt(o, a, b, op):
                return gp.tensor_tensor(o, a, b, op)

            gp.memset(ident[:], 0.0)
            gp.memset(shift[:], 0.0)
            gp.memset(causal[:], 0.0)
            gp.memset(tri[:], 1.0)
            gp.memset(before[:], 1.0)
            gp.memset(head8[:], 16.0 ** -0.5)
            gp.memset(head16[:], 8.0 ** -0.5)
            gp.memset(minus_half[:], -0.5)
            gp.memset(ln_eps[:], LN_EPS)
            gp.memset(minus_round[:], -ROUND)
            gp.memset(ones[:], 1.0)
            gp.drain()
            gp.affine_select(out=ident[:], in_=ident[:], compare_op=ALU.not_equal, fill=1.0, base=0,
                            pattern=[[-1, P]], channel_multiplier=1)
            gp.affine_select(out=shift[:], in_=shift[:], compare_op=ALU.not_equal, fill=1.0, base=-1,
                            pattern=[[1, P]], channel_multiplier=-1)
            for b in range(2):
                half = causal[64 * b:64 * b + 64, :]
                gp.drain()
                gp.affine_select(out=half, in_=half, compare_op=ALU.is_ge, fill=NEG, base=0,
                                pattern=[[-1, ROW]], channel_multiplier=1)
            gp.drain()
            gp.affine_select(out=tri[:], in_=tri[:], compare_op=ALU.is_ge, fill=0.0, base=0,
                            pattern=[[1, ROW]], channel_multiplier=-1)
            gp.drain()
            gp.affine_select(out=before[:], in_=before[:], compare_op=ALU.is_gt, fill=0.0, base=0,
                            pattern=[[1, E], [-1, E]], channel_multiplier=0)
            gp.affine_select(out=head8[:], in_=head8[:], compare_op=ALU.is_ge, fill=0.0, base=0,
                            pattern=[[-16, 8]], channel_multiplier=1)
            gp.affine_select(out=head16[:], in_=head16[:], compare_op=ALU.is_ge, fill=0.0, base=0,
                            pattern=[[-8, 16]], channel_multiplier=1)
            gp.iota(position[:], pattern=[[1, ROW]], base=0, channel_multiplier=0,
                   allow_small_or_imprecise_dtypes=True)
            for b in range(2):
                gp.drain()
                gp.iota(patch_row[64 * b:64 * b + 64, :], pattern=[[0, 1]], base=0, channel_multiplier=1,
                       allow_small_or_imprecise_dtypes=True)
            gp.drain()
            gp.affine_select(out=head8[:], in_=head8[:], compare_op=ALU.is_ge, fill=0.0, base=15,
                            pattern=[[16, 8]], channel_multiplier=-1)
            gp.affine_select(out=head16[:], in_=head16[:], compare_op=ALU.is_ge, fill=0.0, base=7,
                            pattern=[[8, 16]], channel_multiplier=-1)
            gp.memset(shift[:, 64:65], 0.0)
            gp.tensor_copy(ident_bf[:], ident[:])
            gp.memset(ht_shift[:], 0.0)
            gp.memset(v8[:], 1.0)
            gp.memset(v16[:], 1.0)
            gp.memset(pick[:], 0.0)
            gp.drain().then_inc(signal("consts"), 1)
            pool.wait_ge(signal("setup_dve"), 1)

            def part(n_part, g, it, ahead):
                mine = (g,)
                pair = slice(g, g + 1)

                def sg(name):
                    return signal(name, g)

                def tile(name, s):
                    pool.wait_ge(sg(name), reached(name, it, ahead))

                def inv_root(n, o, i):
                    yield f"{n}_rstd"
                    pool.wait_ge(sg(f"{n}_var"), reached(f"{n}_var", it, ahead))
                    power = minus_half[:, 0:o.free_size()]
                    if len(o.shape) > 2:
                        power = power.rearrange("p (a b) -> p a b", a=1)
                    tt(o, i, power, ALU.pow).then_inc(sg(f"{n}_rstd"), 1)

                def inv_std(n):
                    yield f"{n}_rstd"
                    pool.wait_ge(sg(f"{n}_var"), reached(f"{n}_var", it, ahead))
                    tt(var_eps[:, pair], mv[:, pair, 1], ln_eps[:], ALU.add)
                    gp.drain()
                    tt(rstd[:, pair], var_eps[:, pair], minus_half[:, 0:1], ALU.pow).then_inc(sg(f"{n}_rstd"), 1)

                def residual_bias(n, block_name, of):
                    yield f"{block_name}_xb"
                    for s in mine:
                        tile(f"{block_name}_y", s)
                        tt(x[:, s, :], of[:, s, :], bias[:, n, :], ALU.add).then_inc(sg(f"{block_name}_xb"), 1)

                def spread_heads(n, src, table, heads, wait, row=None):
                    yield f"{n}_spread"
                    for s in mine:
                        tile(wait, s)
                        if row is None:
                            to = wide_a[:, s, :].rearrange("p (b h t) -> p b h t", b=2, h=heads)
                            for b in range(2):
                                i = tt(to[:, b], bc(src[:, s, 64 * b:64 * b + 64], 1, heads),
                                       bc(table[:], 2, ROW), ALU.mult)
                        else:
                            to = wide_a[:, s, :].rearrange("p (h t) -> p h t", h=heads)
                            i = tt(to, bc(src[:, s, 64 * row:64 * row + 64], 1, heads),
                                   bc(table[:], 2, ROW), ALU.mult)
                        i.then_inc(sg(f"{n}_spread"), 1)

                def less_max(n):
                    yield f"{n}_sub"
                    tile(f"{n}_max", g)
                    scores = wide_b[:, g, 0:BANK].rearrange("p (h k) -> p h k", h=8)
                    tt(scores, scores, bc(mx[:, g, 0:8], 2, ROW), ALU.subtract).then_inc(sg(f"{n}_sub"), 1)

                def layer_front(L):
                    n = f"l0f{L}"
                    yield from inv_root(f"{n}n", rden[:, pair, :], den[:, pair, :])
                    yield f"{n}_rot"
                    for s in mine:
                        tile(f"{n}_turned", s)
                        tt(wide_a[:, s, :], wide_a[:, s, :], wide_b[:, s, :], ALU.add).then_inc(
                            sg(f"{n}_rot"), 1)
                    yield from less_max(n)

                def layer_back(L):
                    n = f"l0f{L}"
                    yield from inv_std(n)
                    yield f"{n}_yb"
                    for s in mine:
                        tile(f"{n}_y", s)
                        tt(y[:, s, :], y[:, s, :], b_2[:, L, :], ALU.add).then_inc(sg(f"{n}_yb"), 1)

                if n_part == 0:
                    yield "l0a_neg"
                    for s in mine:
                        pool.wait_ge(signal(f"tile_in{s}"), loaded(it, ahead, TILE_LOADS))
                        settle(pool, "pool_waits")
                        gp.tensor_scalar(neg0[:, s, :], mask_row[:, s, :], 0.0, NEG, ALU.is_equal, ALU.mult
                                         ).then_inc(sg("l0a_neg"), 1)
                    yield from inv_std("l0a")
                    yield from inv_root("patch", ctx_sq[:, pair], ctx_sq[:, pair])
                    yield "l0a_xb"
                    for s in mine:
                        pool.wait_ge(signal(f"mask_col_in{s}"), loaded(it, ahead, 16))
                    yield from residual_bias(0, "l0a", xin)
                    yield from spread_heads("l0a", qt, head8, 8, "l0a_qk")
                    yield from less_max("l0a")
                    yield from inv_std("l0f")
                    yield from layer_front(0)
                    return
                if n_part == 1:
                    yield from layer_back(0)
                    yield from layer_front(1)
                    return
                if n_part == 2:
                    yield from layer_back(1)
                    yield "l2a_neg"
                    for s in mine:
                        pool.wait_ge(signal(f"tile_in{s}"), loaded(it, ahead, TILE_LOADS))
                        settle(pool, "pool_waits")
                        gp.tensor_scalar(neg2[:, s, :], mask_i[:, s, :], -1.0, 1.0, ALU.mult, ALU.add)
                    gp.drain()
                    for s in mine:
                        gp.tensor_scalar(neg2[:, s, :], neg2[:, s, :], NEG, None, ALU.mult)
                    gp.drain()
                    for s in mine:
                        gp.tensor_scalar(neg2[:, s, :], neg2[:, s, :], logit_b[:, 0:1], None, ALU.add
                                         ).then_inc(sg("l2a_neg"), 1)
                    yield from inv_std("l1a")
                    yield from inv_root("l1am", small2[:, pair], small[:, pair])
                    yield from residual_bias(1, "l1a", x)
                    yield from inv_std("l1f")
                    yield "l2a_v"
                    for s in mine:
                        gp.tensor_copy(v8[:, s, :, 0:16],
                                       ctx_s[:, s, D:CTX].rearrange("p (h e) -> p h e", h=8)).then_inc(sg("l2a_v"), 1)
                    yield from inv_std("l2a")
                    yield from spread_heads("l2a", ht, head8, 8, "l2a_ht")
                    yield "l3_ctx"
                    for s in mine:
                        for b in range(2):
                            gp.tensor_copy(k_cat[:, s, b, 0, :], ctx_t[:, s, 0, 64 * b:64 * b + 64])
                    gp.drain()
                    for s in mine:
                        for b in range(2):
                            i = gp.tensor_copy(v16[0:64, s, b, :, 0:8],
                                               ctx_v[:, s, b, :].rearrange("p (h e) -> p h e", h=16))
                        i.then_inc(sg("l3_ctx"), 1)
                    gp.drain()
                    yield from less_max("l2a")
                    yield "l3_ctx_used"
                    for s in mine:
                        tile("l2a_o", s)
                        pool.sem_inc(sg("l3_ctx_used"), 1)
                    yield from inv_std("l2f")
                    yield from residual_bias(2, "l2f", x)
                    return
                yield from inv_std("l3a")
                yield from residual_bias(3, "l3a", x)
                for b in range(2):
                    yield from spread_heads(f"l3a{b}", qt, head16, 16, ("l3a_qk", "l3a0_pv")[b], row=b)
                yield from inv_std("l3f")

            all_passes(pool, part)

        @block.scalar
        def _(act):
            a = nc.scalar
            act.wait_ge(signal("weights_in"), 16 * len(once))
            a.activation(gate[:], gate_in[:], ACT.Tanh).then_inc(signal("gates"), 1)

            def part(n_part, g, it, ahead):
                mine = (g,)

                def sg(name):
                    return signal(name, g)

                def tile(name, s):
                    act.wait_ge(sg(name), reached(name, it, ahead))

                def move(wait, done, to, of):
                    yield done
                    for s in mine:
                        tile(wait, s)
                        a.copy(to(s), of(s)).then_inc(sg(done), 1)

                def low(buf):
                    return lambda s: buf[:, s, 0:BANK]

                def exps(n, width):
                    yield f"{n}_exp"
                    for s in mine:
                        tile(f"{n}_sub", s)
                        a.activation(wide_b[:, s, 0:width], wide_b[:, s, 0:width], ACT.Exp).then_inc(
                            sg(f"{n}_exp"), 1)

                def quantised(n, k):
                    if k > 1:
                        yield f"{n}_q"
                        for s in mine:
                            tile(f"{n}_rounded", s)
                            a.activation(quant[:, s, :], wide_c[:, s, :HID], ACT.Identity,
                                         bias=minus_round[:, 0:1]).then_inc(sg(f"{n}_q"), 1)
                    yield f"{n}_qts"
                    for s in mine:
                        tile(f"{n}_qt", s)
                        a.copy(quant_t[:, s, 0:k * P], ps(s, 0, k * P // 2).bitcast(BF16)).then_inc(
                            sg(f"{n}_qts"), 1)

                def layer_front(L):
                    n = f"l0f{L}"
                    yield f"{n}_hs"
                    for s in mine:
                        tile(f"{n}_yt", s)
                        a.copy(ht_shift[0:64, s, :, :], ps(s, 0, P)[0:64].rearrange("p (b t) -> p b t", b=2))
                        a.copy(ht_shift[64:128, s, :, 1:ROW],
                               ps(s, 0, P)[64:128].rearrange("p (b t) -> p b t", b=2)[:, :, 0:ROW - 1]
                               ).then_inc(sg(f"{n}_hs"), 1)
                    yield f"{n}_sq"
                    for s in mine:
                        tile(f"{n}_qk", s)
                        a.activation(wide_c[:, s, :], ps(s), ACT.Square).then_inc(sg(f"{n}_sq"), 1)
                    yield from move(f"{n}_v", f"{n}_vs", lambda s: wide_c[:, s, :], lambda s: ps(s))
                    yield from move(f"{n}_qkt", f"{n}_qts", lambda s: wide_a[:, s, :], lambda s: ps(s))
                    yield from exps(n, BANK)

                def layer_back(L):
                    n = f"l0f{L}"
                    yield from move(f"{n}_pt", f"{n}_pts", low(wide_a), lambda s: ps(s, 0, BANK))
                    yield from move(f"{n}_ot", f"{n}_ots", low(wide_a), lambda s: ps(s, 0, BANK))
                    yield from move(f"{n}_sh", f"{n}_h2", lambda s: h_in[:, s, 64:128], lambda s: ps(s, 0, 64))
                    yield f"{n}_lts"
                    for s in mine:
                        tile(f"{n}_lt", s)
                        a.activation(ht[:, s, :], ps(s, 0, P), ACT.Identity, scale=ln_g[:, L:L + 1],
                                     bias=ln_b[:, L:L + 1]).then_inc(sg(f"{n}_lts"), 1)
                    yield f"{n}_bent"
                    for s in mine:
                        tile(f"{n}_hid", s)
                        for c in range(FFC):
                            i = a.activation(wide_b[:, s, c * P:c * P + P], ps(s, BANK + c * P, P), ACT.Gelu,
                                             bias=b_1[:, L, 1, c:c + 1])
                        i.then_inc(sg(f"{n}_bent"), 1)

                if n_part == 0:
                    yield "patch_sq"
                    for s in mine:
                        act.wait_ge(signal(f"tile_in{s}"), loaded(it, ahead, TILE_LOADS))
                        a.activation(wide_c[:, s, 0:CTX], ctx_s[:, s, :], ACT.Square,
                                     accum_out=ctx_sq[:, s:s + 1]).then_inc(sg("patch_sq"), 1)
                    yield from move("l0a_yt", "l0a_ht", lambda s: ht[:, s, :], lambda s: ps(s, 0, P))
                    yield from exps("l0a", BANK)
                    yield from move("l0a_pt", "l0a_pts", low(wide_c), lambda s: ps(s, BANK, BANK))
                    yield from move("l0a_ot", "l0a_ots", lambda s: qt[:, s, :], lambda s: ps(s, 0, P))
                    yield from layer_front(0)
                    return
                if n_part == 1:
                    yield from layer_back(0)
                    yield from layer_front(1)
                    return
                if n_part == 2:
                    yield from layer_back(1)
                    yield "l1a_power"
                    for s in mine:
                        tile("l1a_decay", s)
                        a.activation(decay[:, s, :], decay[:, s, :], ACT.Exp, scale=-PATCH_DT).then_inc(
                            sg("l1a_power"), 1)
                    yield from move("l1a_yt", "l1a_ht", lambda s: ht[:, s, :], lambda s: ps(s, 0, P))
                    yield from move("l1f_yt", "l1f_ht", lambda s: ht[:, s, :], lambda s: ps(s, 0, P))
                    yield "l1f_exp"
                    pair = slice(g, g + 1)
                    act.wait_ge(sg("l1f_less"), reached("l1f_less", it, ahead))
                    a.activation(rank_b[:, pair, 0, :], logits[:, pair, :], ACT.Exp).then_inc(sg("l1f_exp"), 1)
                    yield from move("l1f_ot", "l1f_ots", lambda s: ht[:, s, :], lambda s: ps(s, 0, P))
                    yield from move("l2a_yt", "l2a_ht", lambda s: ht[:, s, :], lambda s: ps(s, 0, P))
                    yield from exps("l2a", BANK)
                    yield from move("l2a_pt", "l2a_pts", low(wide_c), lambda s: ps(s, BANK, BANK))
                    yield from quantised("l2f", 1)
                    yield "l2f_bent"
                    for s in mine:
                        tile("l2f_pre", s)
                        a.activation(wide_b[:, s, 0:HID], wide_a[:, s, 0:HID], ACT.Gelu).then_inc(sg("l2f_bent"), 1)
                    yield from quantised("l2g", 4)
                    return
                yield from move("l3a_yt", "l3a_ht", lambda s: ht[:, s, :], lambda s: ps(s, 0, P))
                yield "l3a_qk"
                for s in mine:
                    tile("l3a_qkv", s)
                    a.copy(qt[:, s, :], ps(s, 0, P))
                    a.copy(k_cat[:, s, :, 1, :], ps(s, P, P).rearrange("p (b t) -> p b t", b=2)).then_inc(
                        sg("l3a_qk"), 1)
                for b in range(2):
                    yield from exps(f"l3a{b}", 2 * BANK)
                    yield from move(f"l3a{b}_pt", f"l3a{b}_pts", lambda s: wide_c[:, s, :], lambda s: ps(s))
                yield from move("l3a_ot", "l3a_ots", lambda s: qt[:, s, :], lambda s: ps(s, 0, P))
                yield from quantised("l3f", 1)
                yield from move("l3f_st", "l3f_sts", lambda s: scale_t[:, s, :], lambda s: ps(s, BANK, P))
                yield "l3f_bent"
                for s in mine:
                    tile("l3f_conv", s)
                    a.activation(wide_b[:, s, 0:HID], wide_b[:, s, 0:HID], ACT.Silu).then_inc(sg("l3f_bent"), 1)
                yield from quantised("l3g", 4)

            all_passes(act, part)

        @block.vector
        def _(dve):
            v = nc.vector
            tt, ts, stt = v.tensor_tensor, v.tensor_scalar, v.scalar_tensor_tensor

            dve.wait_ge(signal("lens_in"), 16)
            v.tensor_copy(lens[:], lens_i[:]).then_inc(signal("lens_f"), 1)
            dve.wait_ge(signal("cum"), 1)
            dve.wait_ge(signal("consts"), 1)
            ts(last[:], ps(0, 0, ROW)[0:B], -1.0, None, ALU.add)
            v.drain()
            ts(wrap[:], last[:], 0.0, float(ROW), ALU.is_lt, ALU.mult)
            v.drain()
            tt(last[:], last[:], wrap[:], ALU.add)
            v.drain()
            hit = wide_a[0:B, :, :].rearrange("p g w -> p (g w)").rearrange("p (l j) -> p l j", l=ROW)
            tt(hit, bc(last[:], 1, ROW), bc(position[:], 2, ROW), ALU.is_equal)
            v.drain()
            v.tensor_reduce(bound[:], hit, AX.X, ALU.max).then_inc(signal("bound"), 1)
            dve.wait_ge(signal("bound_tp"), 1)
            v.tensor_copy(bound_t[:], ps(0, 0, B)[0:ROW]).then_inc(signal("bound_ts"), 1)
            dve.wait_ge(signal("plug_p"), 1)
            ts(plug_all[:], ps(0, 0, ROW)[0:B], -1.0, 0.0, ALU.add, ALU.max)
            v.drain().then_inc(signal("plug_made"), 1)

            dve.wait_ge(signal("weights_in"), 16 * len(once))
            dve.wait_ge(signal("gates"), 1)
            for n, of in enumerate((0, 1, 6, 3)):
                ts(bias[:, n, :], bias_in[:, n, :], gate[:, of:of + 1], None, ALU.mult)
            ts(w_in[:], w_in[:], g_res[:, 0:1], None, ALU.mult)
            for L in range(2):
                for qk in range(2):
                    tt(turn[:, L, qk, 0, :], rotary[:, qk, 0, :], qk_scale[:, L, qk, :], ALU.mult)
                    for half in range(2):
                        tt(turn[:, L, qk, 1, 32 * half:32 * half + 32],
                           rotary[:, qk, 1, 32 * half:32 * half + 32],
                           qk_scale[:, L, qk, 32 - 32 * half:64 - 32 * half], ALU.mult)
            v.tensor_reduce(tern_sum[:], raw[:], AX.X, ALU.add, apply_absolute_value=True)
            v.drain().then_inc(signal("tern_rows"), 1)
            dve.wait_ge(signal("tern_all"), 1)
            ts(tern_step[:], ps(0, 0, 4), 1.0 / (P * HID), LN_EPS, ALU.mult, ALU.max)
            v.drain()
            v.reciprocal(tern_inv[:], tern_step[:])
            ts(tern_127[:], tern_step[:], 1.0 / 127.0, None, ALU.mult)
            v.drain()
            for n, of in ((1, 6), (3, 7)):
                ts(tern_127[:, n:n + 1], tern_127[:, n:n + 1], gate[:, of:of + 1], None, ALU.mult)
            for n in range(4):
                ts(raw[:, n, :], raw[:, n, :], tern_inv[:, n:n + 1], ROUND, ALU.mult, ALU.add)
            v.drain()
            for n in range(4):
                ts(raw[:, n, :], raw[:, n, :], -ROUND, 1.0, ALU.add, ALU.min)
            v.drain()
            for n in range(4):
                ts(tern[:, n, :], raw[:, n, :], -1.0, None, ALU.max)
            v.drain().then_inc(signal("setup_dve"), 1)

            def part(n_part, g, it, ahead):
                mine = (g,)
                pair = slice(g, g + 1)

                def sg(name):
                    return signal(name, g)

                def tile(name, s):
                    dve.wait_ge(sg(name), reached(name, it, ahead))

                def statistics(n, of):
                    yield f"{n}_var"
                    if n != "l0a":
                        v.drain()
                    if n in ("l0f0", "l0f1"):
                        tile(f"{n}_h2", g)
                    for s in mine:
                        v.bn_stats(stats[:, s, :], of[:, s, :])
                    v.drain()
                    for s in mine:
                        v.bn_aggr(mv[:, s, :], stats[:, s, :]).then_inc(sg(f"{n}_var"), 1)

                def normalise(n, to, of, by=None):
                    yield f"{n}_y"
                    by = rstd if by is None else by
                    tile(f"{n}_rstd" if by is rstd else "l1am_rstd", g)
                    if by is not rstd:
                        tt(by[:, pair], rstd[:, pair], small2[:, pair], ALU.mult)
                        v.drain()
                    for s in mine:
                        ts(to[:, s, :], of[:, s, :], mv[:, s, 0:1], by[:, s:s + 1], ALU.subtract, ALU.mult
                           ).then_inc(sg(f"{n}_y"), 1)

                def layer_norm(n, of=x):
                    yield from statistics(n, of)
                    yield from normalise(n, y, of)

                def softmax_max(n, neg):
                    yield f"{n}_max"
                    tile(f"{n}_sc", g)
                    neg(g)
                    v.drain()
                    v.tensor_reduce(mx[:, g, 0:8], grouped(g, 8, ROW), AX.X, ALU.max).then_inc(sg(f"{n}_max"), 1)

                def softmax_less_max(n, of):
                    yield f"{n}_sub"
                    tile(f"{n}_sc", g)
                    v.tensor_reduce(mx[:, g, 0:8], of, AX.X, ALU.max)
                    v.drain()
                    tt(wide_b[:, g, :].rearrange("p (g k) -> p g k", g=8), of, bc(mx[:, g, 0:8], 2, P),
                       ALU.subtract).then_inc(sg(f"{n}_sub"), 1)

                def grouped(s, groups, keys):
                    return wide_b[:, s, 0:groups * keys].rearrange("p (g k) -> p g k", g=groups)

                def divide_heads(n, to):
                    def part(s, b):
                        return ps(s, b * BANK, 8 * 17)[64 * b:64 * b + 64].rearrange("p (h e) -> p h e", h=8)
                    yield f"{n}_o"
                    for s in mine:
                        tile(f"{n}_pv", s)
                        for b in range(2):
                            v.reciprocal(rden[64 * b:64 * b + 64, s, 0:8], part(s, b)[:, :, 16])
                    v.drain()
                    for s in mine:
                        for b in range(2):
                            i = tt(to[64 * b:64 * b + 64, s, :].rearrange("p (h e) -> p h e", h=8),
                                   part(s, b)[:, :, 0:16],
                                   bc(rden[64 * b:64 * b + 64, s, 0:8], 2, 16), ALU.mult)
                        i.then_inc(sg(f"{n}_o"), 1)

                def update(n, col, at, bias_done=None):
                    yield f"{n}_x"
                    for s in mine:
                        tile(f"{n}_out", s)
                        if bias_done:
                            tile(bias_done, s)
                        stt(x[:, s, :], ps(s, at, D), gate[:, col:col + 1], x[:, s, :], ALU.mult, ALU.add
                            ).then_inc(sg(f"{n}_x"), 1)

                def add_neg(neg):
                    def go(s):
                        tt(wide_b[:, s, 0:BANK].rearrange("p (g k) -> p g k", g=4),
                           ps(s, 0, BANK).rearrange("p (g k) -> p g k", g=4), bc(neg[:, s, :], 1, 4), ALU.add)
                    return go

                def quantise(n, of, width, step, wait=None):
                    yield f"{n}_rounded" if width == HID else f"{n}_q"
                    v.drain()
                    for s in mine:
                        if wait:
                            tile(wait, s)
                        v.tensor_reduce(small[:, s:s + 1], of(s), AX.X, ALU.max, apply_absolute_value=True)
                    v.drain()
                    ts(small2[:, pair], small[:, pair], LN_EPS, 1.0 / 127.0, ALU.max, ALU.mult)
                    v.drain()
                    v.reciprocal(small2[:, pair], small2[:, pair])
                    ts(small[:, pair], small[:, pair], LN_EPS, tern_127[:, step:step + 1], ALU.max, ALU.mult)
                    v.drain()
                    for s in mine:
                        i = ts(wide_c[:, s, 0:width], of(s), small2[:, s:s + 1], ROUND, ALU.mult, ALU.add)
                    if width == HID:
                        i.then_inc(sg(f"{n}_rounded"), 1)
                        return
                    v.drain()
                    for s in mine:
                        ts(quant[:, s, 0:width], wide_c[:, s, 0:width], -ROUND, None, ALU.add
                           ).then_inc(sg(f"{n}_q"), 1)

                def update_scaled(n, bias_done=None):
                    yield f"{n}_x"
                    for s in mine:
                        tile(f"{n}_out", s)
                        if bias_done:
                            tile(bias_done, s)
                        stt(x[:, s, :], ps(s, BANK, D), small[:, s:s + 1], x[:, s, :], ALU.mult, ALU.add
                            ).then_inc(sg(f"{n}_x"), 1)

                def layer_front(L):
                    n = f"l0f{L}"
                    yield f"{n}_turned"
                    for s in mine:
                        tile(f"{n}_sq", s)
                        v.tensor_reduce(den[:, s, :], wide_c[:, s, :].rearrange("p (g e) -> p g e", g=16),
                                        AX.X, ALU.add)
                        src = ps(s).rearrange("p (q h e) -> p q h e", q=2, h=8)
                        cos = wide_a[:, s, :].rearrange("p (q h e) -> p q h e", q=2, h=8)
                        sin = wide_b[:, s, :].rearrange("p (q h e) -> p q h e", q=2, h=8)
                        for q in range(2):
                            tt(cos[:, q], src[:, q], bc(turn[:, L, q, 0, :], 1, 8), ALU.mult)
                            for half in range(2):
                                lo, hi = 32 * half, 32 - 32 * half
                                i = tt(sin[:, q, :, lo:lo + 32], src[:, q, :, hi:hi + 32],
                                       bc(turn[:, L, q, 1, lo:lo + 32], 1, 8), ALU.mult)
                        i.then_inc(sg(f"{n}_turned"), 1)
                    yield f"{n}n_var"
                    v.drain()
                    ts(den[:, pair, :], den[:, pair, :], 1e-24, None, ALU.max).then_inc(sg(f"{n}n_var"), 1)
                    yield f"{n}_qkn"
                    tile(f"{n}n_rstd", g)
                    for s in mine:
                        tile(f"{n}_rot", s)
                        tt(wide_b[:, s, :].rearrange("p (g e) -> p g e", g=16),
                           wide_a[:, s, :].rearrange("p (g e) -> p g e", g=16),
                           bc(rden[:, s, :], 2, ROW), ALU.mult).then_inc(sg(f"{n}_qkn"), 1)
                    def add_causal(s):
                        for h2 in range(2):
                            tt(grouped(s, 8, ROW)[:, 4 * h2:4 * h2 + 4],
                               ps(s, h2 * BANK, 256).rearrange("p (g k) -> p g k", g=4),
                               bc(causal[:], 1, 4), ALU.add)

                    yield from softmax_max(n, add_causal)

                def layer_back(L):
                    n = f"l0f{L}"
                    yield f"{n}_pt"
                    for s in mine:
                        tile(f"{n}_exp", s)
                        v.tensor_reduce(den[:, s, 0:8], grouped(s, 8, ROW), AX.X, ALU.add)
                    v.drain()
                    v.reciprocal(rden[:, pair, 0:8], den[:, pair, 0:8])
                    yield f"{n}_o"
                    v.drain()
                    for s in mine:
                        tile(f"{n}_pv", s)
                        o = wide_b[:, s, 0:BANK].rearrange("p (j k e) -> p j k e", j=4, k=2)
                        for k in range(2):
                            i = tt(o[:, :, k, :], ps(s, k * BANK, 256).rearrange("p (j e) -> p j e", j=4),
                                   bc(rden[:, s, 0:8].rearrange("p (j k) -> p j k", k=2)[:, :, k], 2, ROW),
                                   ALU.mult)
                        i.then_inc(sg(f"{n}_o"), 1)
                    yield f"{n}_y1"
                    for s in mine:
                        tile(f"{n}_wo", s)
                        tt(y[:, s, :], ps(s, BANK, D), y[:, s, :], ALU.add).then_inc(sg(f"{n}_y1"), 1)
                    yield f"{n}_sh"
                    v.drain()
                    for s in mine:
                        v.tensor_copy(h_in[:, s, 0:64], y[:, s, 0:64])
                    yield from statistics(n, h_in)
                    yield from normalise(n, h_in, h_in)
                    yield f"{n}_gated"
                    for s in mine:
                        tile(f"{n}_bent", s)
                        for c in range(FFC):
                            i = stt(wide_a[:, s, c * P:c * P + P], ps(s, c * P, P), b_1[:, L, 0, c:c + 1],
                                    wide_b[:, s, c * P:c * P + P], ALU.add, ALU.mult)
                        i.then_inc(sg(f"{n}_gated"), 1)
                    yield f"{n}_x"
                    for s in mine:
                        tile(f"{n}_out", s)
                        tile(f"{n}_yb", s)
                        tt(y[:, s, :], ps(s, BANK, D), y[:, s, :], ALU.add).then_inc(sg(f"{n}_x"), 1)

                if n_part == 0:
                    yield "l0a_var"
                    for s in mine:
                        dve.wait_ge(signal(f"tile_in{s}"), loaded(it, ahead, TILE_LOADS))
                    yield from statistics("l0a", xin)
                    yield "patch_var"
                    tile("patch_sq", g)
                    v.tensor_scalar(ctx_sq[:, pair], ctx_sq[:, pair], 1.0 / CTX, LN_EPS, ALU.mult, ALU.add).then_inc(
                        sg("patch_var"), 1)
                    yield from normalise("l0a", y, xin)
                    yield "l0a_qk"
                    for s in mine:
                        tile("l0a_qkv", s)
                        dve.wait_ge(signal(f"mask_col_in{s}"), loaded(it, ahead, 16))
                        stt(qt[:, s, :], ps(s, 0, P), b_q[:, 0:1], mask_row[:, s, :], ALU.add, ALU.mult)
                        stt(kt[:, s, :], ps(s, P, P), b_k[:, 0:1], mask_row[:, s, :], ALU.add, ALU.mult
                            ).then_inc(sg("l0a_qk"), 1)
                        tt(vtmp[:, s, :], ps(s, BANK, D), b_v[:], ALU.add)
                    v.drain()
                    for s in mine:
                        ts(v8[:, s, :, 0:16], vtmp[:, s, :].rearrange("p (h e) -> p h e", h=8), mask_col[:, s, :],
                           None, ALU.mult).then_inc(sg("l0a_v"), 1)
                    yield "patches"
                    tile("patch_rstd", g)
                    for s in mine:
                        stt(patches[:, s, :], ctx_s[:, s, 0:D], ctx_sq[:, s:s + 1], g_init[:], ALU.mult, ALU.mult
                            ).then_inc(sg("patches"), 1)

                    yield "l0a_max"
                    tile("l0a_neg", g)
                    yield from softmax_max("l0a", add_neg(neg0))
                    yield from divide_heads("l0a", vtmp)
                    yield from update("l0a", 0, BANK, "l0a_xb")

                    yield from layer_norm("l0f")
                    yield from layer_front(0)
                    return
                if n_part == 1:
                    yield from layer_back(0)
                    yield from layer_front(1)
                    return
                if n_part == 2:
                    yield from layer_back(1)
                    v.drain()
                    for s in mine:
                        stt(x[:, s, :], y[:, s, :], gate[:, 4:5], x[:, s, :], ALU.mult, ALU.add)
                    yield from statistics("l1a", x)
                    yield "l1am_var"
                    tile("l1a_rstd", g)
                    tt(small[:, pair], mv[:, pair, 1], rstd[:, pair], ALU.mult)
                    v.drain()
                    tt(small[:, pair], small[:, pair], rstd[:, pair], ALU.mult)
                    v.drain()
                    ts(small[:, pair], small[:, pair], LN_EPS, None, ALU.add).then_inc(sg("l1am_var"), 1)
                    yield "l1a_decay"
                    for s in mine:
                        dve.wait_ge(signal(f"plug_in{s}"), loaded(it, ahead, 32))
                        ts(decay[:, s, :], plug[:, s, :], patch_row[:, 0:1], 0.0, ALU.subtract, ALU.max
                           ).then_inc(sg("l1a_decay"), 1)
                        ts(reach[:, s, :], plug[:, s, :], patch_row[:, 0:1], PATCH_B, ALU.is_ge, ALU.mult)
                    yield from normalise("l1a", y, x, small)
                    yield "l1a_pick"
                    for s in mine:
                        tile("l1a_power", s)
                        for b in range(2):
                            r = slice(64 * b, 64 * b + 64)
                            i = tt(pick[r, s, b, :], decay[r, s, :], reach[r, s, :], ALU.mult)
                        i.then_inc(sg("l1a_pick"), 1)
                    yield from update("l1a", 1, BANK, "l1a_xb")

                    yield from layer_norm("l1f")
                    yield "l1f_less"
                    for s in mine:
                        tile("l1f_lg", s)
                        v.tensor_copy(logits[:, s, :], ps(s, 0, E))
                    v.drain()
                    tt(rank_a[:, pair], bc(logits[:, pair], 2, E), bc(logits[:, pair], 3, E), ALU.is_gt)
                    tt(rank_b[:, pair], bc(logits[:, pair], 2, E), bc(logits[:, pair], 3, E), ALU.is_equal)
                    v.tensor_reduce(small[:, pair], logits[:, pair], AX.X, ALU.max)
                    v.drain()
                    for s in mine:
                        tt(rank_b[:, s], rank_b[:, s], before[:], ALU.mult)
                    tt(logits[:, pair], logits[:, pair], bc(small[:, pair], 2, E), ALU.subtract)
                    v.drain()
                    tt(rank_a[:, pair], rank_a[:, pair], rank_b[:, pair], ALU.add)
                    v.drain().then_inc(sg("l1f_less"), 1)
                    yield "l1f_o"
                    v.tensor_reduce(rank[:, pair], rank_a[:, pair], AX.X, ALU.add)
                    v.drain()
                    tile("l1f_exp", g)
                    stt(rank[:, pair], rank[:, pair], 2.0, rank_b[:, pair, 0, :], ALU.is_lt, ALU.mult)
                    v.drain()
                    v.tensor_reduce(small[:, pair], rank[:, pair], AX.X, ALU.add)
                    v.drain()
                    v.reciprocal(small[:, pair], small[:, pair])
                    v.drain()
                    tt(rank[:, pair], rank[:, pair], bc(small[:, pair], 2, E), ALU.mult)
                    v.drain()
                    for s in mine:
                        tt(vtmp[:, s, :].rearrange("p (e r) -> p e r", e=E),
                           ps(s, BANK, P).rearrange("p (e r) -> p e r", e=E), bc(rank[:, s, :], 2, R), ALU.mult
                           ).then_inc(sg("l1f_o"), 1)
                    yield from update("l1f", 5, BANK)

                    yield from layer_norm("l2a")
                    yield "l2a_max"
                    tile("l2a_neg", g)
                    yield from softmax_max("l2a", add_neg(neg2))
                    yield from divide_heads("l2a", vtmp)
                    yield "l3_ctx_used"
                    v.drain()
                    for s in mine:
                        stt(x[:, s, :], vtmp[:, s, :], gate[:, 2:3], x[:, s, :], ALU.mult, ALU.add)

                    yield from layer_norm("l2f")
                    yield from quantise("l2f", lambda s: y[:, s, :], D, 0)
                    yield "l2f_pre"
                    for s in mine:
                        tile("l2f_hid", s)
                        stt(wide_a[:, s, 0:HID], ps(s, BANK, HID), small[:, s:s + 1], b_t1[:], ALU.mult, ALU.add
                            ).then_inc(sg("l2f_pre"), 1)
                    yield from quantise("l2g", lambda s: wide_b[:, s, 0:HID], HID, 1, "l2f_bent")
                    yield from update_scaled("l2g", "l2f_xb")
                    return
                yield from layer_norm("l3a")
                yield "l3a_v"
                for s in mine:
                    tile("l3a_qkv", s)
                    for b in range(2):
                        i = v.tensor_copy(v16[64:128, s, b, :, 0:8],
                                          ps(s, BANK + b * D, D)[64:128].rearrange("p (h e) -> p h e", h=16))
                    i.then_inc(sg("l3a_v"), 1)
                for b in range(2):
                    n = f"l3a{b}"
                    yield from softmax_less_max(n, ps(g).rearrange("p (g k) -> p g k", g=8))
                    def part(s):
                        return ps(s, 0, 16 * 9)[64 * b:64 * b + 64].rearrange("p (h e) -> p h e", h=16)
                    yield f"{n}_o"
                    for s in mine:
                        tile(f"{n}_pv", s)
                        v.reciprocal(rden[64 * b:64 * b + 64, s, :], part(s)[:, :, 8])
                    v.drain()
                    for s in mine:
                        tt(vtmp[64 * b:64 * b + 64, s, :].rearrange("p (h e) -> p h e", h=16),
                           part(s)[:, :, 0:8], bc(rden[64 * b:64 * b + 64, s, :], 2, 8), ALU.mult
                           ).then_inc(sg(f"{n}_o"), 1)
                yield from update("l3a", 3, BANK, "l3a_xb")

                yield from layer_norm("l3f")
                yield from quantise("l3f", lambda s: y[:, s, :], D, 2)
                yield "l3f_diag"
                for s in mine:
                    ts(vtmp[:, s, :], ident[:], small[:, s:s + 1], None, ALU.mult).then_inc(sg("l3f_diag"), 1)
                yield "l3f_conv"
                for s in mine:
                    tile("l3f_hid", s)
                    tile("l3f_sts", s)
                    tt(wide_a[:, s, 0:HID].rearrange("p (c t) -> p c t", c=4),
                       ps(s, 0, HID).rearrange("p (c t) -> p c t", c=4), bc(scale_t[:, s, :], 1, 4), ALU.mult)
                v.drain()

                def chan(buf, s, c):
                    return buf[:, s, c * P:c * P + P].rearrange("p (b t) -> p b t", b=2)
                for s in mine:
                    for c in range(4):
                        ts(chan(wide_b, s, c), chan(wide_a, s, c), conv_w[:, c, 1:2], conv_b[:, c:c + 1],
                           ALU.mult, ALU.add)
                v.drain()
                for s in mine:
                    for c in range(4):
                        to = chan(wide_b, s, c)[:, :, 1:ROW]
                        stt(to, chan(wide_a, s, c)[:, :, 0:ROW - 1], conv_w[:, c, 0:1], to, ALU.mult, ALU.add)
                v.drain()
                for s in mine:
                    for c in range(4):
                        to = chan(wide_b, s, c)[:, :, 0:ROW - 1]
                        i = stt(to, chan(wide_a, s, c)[:, :, 1:ROW], conv_w[:, c, 2:3], to, ALU.mult, ALU.add)
                    i.then_inc(sg("l3f_conv"), 1)
                yield from quantise("l3g", lambda s: ps(s, 0, HID), HID, 3, "l3f_act")
                yield "l3f_x"
                for s in mine:
                    tile("l3g_out", s)
                    stt(x[:, s, :], ps(s, BANK, D), small[:, s:s + 1], x[:, s, :], ALU.mult, ALU.add
                        ).then_inc(sg("l3f_x"), 1)

            all_passes(dve, part)

        @block.tensor
        def _(pe):
            mm = nc.tensor.matmul

            pe.wait_ge(signal("consts"), 1)
            pe.wait_ge(signal("lens_f"), 1)
            mm(ps(0, 0, ROW)[0:B], lens[:], tri[:], start=True, stop=True).then_inc(signal("cum"), 1)
            pe.wait_ge(signal("bound"), 1)
            mm(ps(0, 0, B)[0:ROW], bound[:], ident[0:B, 0:B], start=True, stop=True).then_inc(signal("bound_tp"), 1)
            pe.wait_ge(signal("bound_ts"), 1)
            mm(ps(0, 0, ROW)[0:B], bound_t[:], tri[:], start=True, stop=True).then_inc(signal("plug_p"), 1)
            pe.wait_ge(signal("tern_rows"), 1)
            mm(ps(0, 0, 4), ones[:], tern_sum[:], start=True, stop=True).then_inc(signal("tern_all"), 1)
            pe.wait_ge(signal("setup_dve"), 1)

            def part(n_part, g, it, ahead):
                mine = (g,)
                pair = slice(g, g + 1)

                def sg(name):
                    return signal(name, g)

                def tile(name, s):
                    pe.wait_ge(sg(name), reached(name, it, ahead))

                def turn_over(wait, done, of, at=0):
                    yield done
                    for s in mine:
                        tile(wait, s)
                        nc.tensor.transpose(ps(s, at, P), of(s), ident[:]).then_inc(sg(done), 1)

                def turn_many(wait, done, of, n, at):
                    yield done
                    for s in mine:
                        tile(wait, s)
                        for c in range(n):
                            i = nc.tensor.transpose(ps(s, at + c * P, P), of(s)[:, c * P:c * P + P], ident[:])
                        i.then_inc(sg(done), 1)

                def scores8(n, keys, waits):
                    yield f"{n}_sc"
                    for s in mine:
                        for w in waits:
                            tile(w, s)
                        for b in range(2):
                            for h4 in range(4):
                                i = mm(ps(s, h4 * P + b * ROW, ROW),
                                       wide_a[:, s, b * BANK + h4 * P:b * BANK + h4 * P + P],
                                       keys(s)[:, 64 * b:64 * b + 64], start=True, stop=True)
                        i.then_inc(sg(f"{n}_sc"), 1)

                def values8(n):
                    yield f"{n}_pv"
                    for s in mine:
                        tile(f"{n}_pts", s)
                        tile(f"{n}_v", s)
                        settle(pe, "pe_waits")
                        for hh in range(8):
                            for b in range(2):
                                r = slice(64 * b, 64 * b + 64)
                                i = mm(ps_all[r, s, b * BANK + hh * 17:b * BANK + hh * 17 + 17],
                                       wide_c[r, s, hh * ROW:hh * ROW + ROW], v8[r, s, hh, :],
                                       start=True, stop=True)
                        i.then_inc(sg(f"{n}_pv"), 1)

                def turn_quantised(n, k):
                    yield f"{n}_qt"
                    for s in mine:
                        tile(f"{n}_q", s)
                        for c in range(k):
                            i = nc.tensor.transpose(ps(s, c * P // 2, P // 2).bitcast(BF16),
                                                    quant[:, s, c * P:c * P + P], ident_bf[:])
                        i.then_inc(sg(f"{n}_qt"), 1)

                def down(n, w):
                    yield f"{n}_out"
                    for s in mine:
                        tile(f"{n}_qts", s)
                        for c in range(4):
                            i = mm(ps(s, BANK, D), quant_t[:, s, c * P:c * P + P], tern[:, w, c * P:c * P + P],
                                   start=(c == 0), stop=(c == 3))
                        i.then_inc(sg(f"{n}_out"), 1)

                def layer_front(L):
                    n = f"l0f{L}"
                    yield from turn_over("l0f_y" if L == 0 else "l0f0_x", f"{n}_yt", lambda s: y[:, s, :])
                    yield f"{n}_qk"
                    for s in mine:
                        tile(f"{n}_hs", s)
                        hs = ht_shift[:, s, :, :].rearrange("p b t -> p (b t)")
                        for q in range(2):
                            i = mm(ps(s, q * BANK, BANK), hs, w_qkv[:, L, q * INNER:q * INNER + INNER],
                                   start=True, stop=True)
                        i.then_inc(sg(f"{n}_qk"), 1)
                    yield f"{n}_v"
                    for s in mine:
                        tile(f"{n}_turned", s)
                        for b in range(2):
                            for half in range(2):
                                i = mm(ps_all[64 * half:64 * half + 64, s, b * BANK:b * BANK + BANK],
                                       ht_shift[:, s, b, :], w_qkv[:, L, 2 * INNER:3 * INNER],
                                       start=True, stop=True)
                        i.then_inc(sg(f"{n}_v"), 1)
                    yield f"{n}_qkt"
                    for s in mine:
                        tile(f"{n}_qkn", s)
                        tile(f"{n}_vs", s)
                        for c in range(8):
                            i = nc.tensor.transpose(ps(s, c * P, P), wide_b[:, s, c * P:c * P + P], ident[:])
                        i.then_inc(sg(f"{n}_qkt"), 1)
                    yield f"{n}_sc"
                    for s in mine:
                        tile(f"{n}_qts", s)
                        settle(pe, "pe_waits")
                        for c in range(4):
                            for b in range(2):
                                for h2 in range(2):
                                    r = slice(64 * h2, 64 * h2 + 64)
                                    col = c * P + 64 * b
                                    i = mm(ps_all[64 * b:64 * b + 64, s, h2 * BANK + c * ROW:h2 * BANK + c * ROW + ROW],
                                           wide_a[r, s, col:col + 64], wide_a[r, s, BANK + col:BANK + col + 64],
                                           start=True, stop=True)
                        i.then_inc(sg(f"{n}_sc"), 1)

                def layer_back(L):
                    n = f"l0f{L}"
                    yield from turn_many(f"{n}_exp", f"{n}_pt", lambda s: wide_b[:, s, 0:BANK], 4, 0)
                    yield f"{n}_pv"
                    for s in mine:
                        tile(f"{n}_pts", s)
                        settle(pe, "pe_waits")
                        for j in range(4):
                            for b in range(2):
                                for k in range(2):
                                    head = 4 * (j % 2) + 2 * k + j // 2
                                    r = slice(64 * k, 64 * k + 64)
                                    i = mm(ps_all[64 * b:64 * b + 64, s, k * BANK + j * ROW:k * BANK + j * ROW + ROW],
                                           wide_a[r, s, j * P + 64 * b:j * P + 64 * b + 64],
                                           wide_c[r, s, b * BANK + head * ROW:b * BANK + head * ROW + ROW],
                                           start=True, stop=True)
                        i.then_inc(sg(f"{n}_pv"), 1)
                    yield from turn_many(f"{n}_o", f"{n}_ot", lambda s: wide_b[:, s, 0:BANK], 4, 0)
                    yield f"{n}_wo"
                    for s in mine:
                        tile(f"{n}_ots", s)
                        for c in range(4):
                            i = mm(ps(s, BANK, D), wide_a[:, s, c * P:c * P + P], w_o[:, L, c, :],
                                   start=(c == 0), stop=(c == 3))
                        i.then_inc(sg(f"{n}_wo"), 1)
                    yield f"{n}_sh"
                    for s in mine:
                        tile(f"{n}_y1", s)
                        mm(ps(s, 0, 64), shift[:], y[:, s, 64:128], start=True, stop=True).then_inc(
                            sg(f"{n}_sh"), 1)
                    yield from turn_over(f"{n}_y", f"{n}_lt", lambda s: h_in[:, s, :])
                    yield f"{n}_hid"
                    for s in mine:
                        tile(f"{n}_lts", s)
                        for half in range(2):
                            for c in range(FFC):
                                i = mm(ps(s, half * BANK + c * P, P), w_1[:, L, half, c, :], ht[:, s, :],
                                       start=True, stop=True)
                        i.then_inc(sg(f"{n}_hid"), 1)
                    yield f"{n}_out"
                    for s in mine:
                        tile(f"{n}_gated", s)
                        for c in range(FFC):
                            i = mm(ps(s, BANK, D), wide_a[:, s, c * P:c * P + P], w_2[:, L, c, :],
                                   start=(c == 0), stop=(c == FFC - 1))
                        i.then_inc(sg(f"{n}_out"), 1)

                if n_part == 0:
                    yield from turn_over("l0a_y", "l0a_yt", lambda s: y[:, s, :])
                    yield "l0a_qkv"
                    for s in mine:
                        pe.wait_ge(signal(f"tile_in{s}"), loaded(it, ahead, TILE_LOADS))
                        for c in range(2):
                            mm(ps(s, BANK, D), ctx_t[:, s, c, :], w_src[:, c, D:2 * D], start=(c == 0), stop=(c == 1))
                        tile("l0a_ht", s)
                        mm(ps(s, 0, P), w_tgt[:], ht[:, s, :], start=True, stop=True)
                        for c in range(2):
                            i = mm(ps(s, P, P), w_src[:, c, 0:D], ctx_t[:, s, c, :], start=(c == 0), stop=(c == 1))
                        i.then_inc(sg("l0a_qkv"), 1)
                    yield from scores8("l0a", lambda s: kt[:, s, :], ("l0a_spread", "l0a_v"))
                    yield from turn_many("l0a_exp", "l0a_pt", lambda s: wide_b[:, s, 0:BANK], 4, BANK)
                    yield from values8("l0a")
                    yield from turn_over("l0a_o", "l0a_ot", lambda s: vtmp[:, s, :])
                    yield "l0a_out"
                    for s in mine:
                        tile("l0a_ots", s)
                        mm(ps(s, BANK, D), ht[:, s, :], w_out[:, 0, :], start=True, stop=False)
                        mm(ps(s, BANK, D), qt[:, s, :], w_out[:, 1, :], start=False, stop=True).then_inc(
                            sg("l0a_out"), 1)

                    yield from layer_front(0)
                    return
                if n_part == 1:
                    yield from layer_back(0)
                    yield from layer_front(1)
                    return
                if n_part == 2:
                    yield from layer_back(1)
                    yield from turn_over("l1a_y", "l1a_yt", lambda s: y[:, s, :])
                    yield "l1a_out"
                    for s in mine:
                        tile("l1a_ht", s)
                        tile("l1a_pick", s)
                        mm(ps(s, BANK, D), ht[:, s, :], w_in[:], start=True, stop=False)
                        mm(ps(s, BANK, D), pick[:, s, :, :].rearrange("p b t -> p (b t)"), patches[:, s, :],
                           start=False, stop=True).then_inc(sg("l1a_out"), 1)

                    yield from turn_over("l1f_y", "l1f_yt", lambda s: y[:, s, :])
                    yield "l1f_lg"
                    for s in mine:
                        tile("l1f_ht", s)
                        mm(ps(s, 0, E), ht[:, s, :], w_gate[:], start=True, stop=True)
                        mm(ps(s, BANK, P), ht[:, s, :], w_a[:], start=True, stop=True).then_inc(sg("l1f_lg"), 1)
                    yield from turn_over("l1f_o", "l1f_ot", lambda s: vtmp[:, s, :])
                    yield "l1f_out"
                    for s in mine:
                        tile("l1f_ots", s)
                        mm(ps(s, BANK, D), ht[:, s, :], w_b[:], start=True, stop=True).then_inc(sg("l1f_out"), 1)

                    yield from turn_over("l2a_y", "l2a_yt", lambda s: y[:, s, :])
                    yield from scores8("l2a", lambda s: ctx_t[:, s, 0, :], ("l2a_spread",))
                    yield from turn_many("l2a_exp", "l2a_pt", lambda s: wide_b[:, s, 0:BANK], 4, BANK)
                    yield from values8("l2a")

                    yield from turn_quantised("l2f", 1)
                    yield "l2f_hid"
                    for s in mine:
                        tile("l2f_qts", s)
                        mm(ps(s, BANK, HID), quant_t[:, s, 0:P], tern[:, 0, :], start=True, stop=True).then_inc(
                            sg("l2f_hid"), 1)
                    yield from turn_quantised("l2g", 4)
                    yield from down("l2g", 1)
                    return
                yield from turn_over("l3a_y", "l3a_yt", lambda s: y[:, s, :])
                yield "l3a_qkv"
                for s in mine:
                    tile("l3a_ht", s)
                    for q in range(2):
                        mm(ps(s, q * P, P), w_qkv3[:, q * D:q * D + D], ht[:, s, :], start=True, stop=True)
                    for b in range(2):
                        i = mm(ps_all[64:128, s, BANK + b * D:BANK + b * D + D], ht[:, s, 64 * b:64 * b + 64],
                               w_qkv3[:, 2 * D:3 * D], start=True, stop=True)
                    i.then_inc(sg("l3a_qkv"), 1)
                for b in range(2):
                    n = f"l3a{b}"
                    yield f"{n}_sc"
                    for s in mine:
                        tile(f"{n}_spread", s)
                        if b == 0:
                            tile("l3a_v", s)
                            tile("l3_ctx", s)
                        else:
                            tile("l3a0_o", s)
                        for c in range(8):
                            i = mm(ps(s, c * P, P), wide_a[:, s, c * P:c * P + P],
                                   k_cat[:, s, b, :, :].rearrange("p a t -> p (a t)"), start=True, stop=True)
                        i.then_inc(sg(f"{n}_sc"), 1)
                    yield from turn_many(f"{n}_exp", f"{n}_pt", lambda s: wide_b[:, s, :], 8, 0)
                    yield f"{n}_pv"
                    for s in mine:
                        tile(f"{n}_pts", s)
                        for hh in range(16):
                            i = mm(ps_all[64 * b:64 * b + 64, s, hh * 9:hh * 9 + 9],
                                   wide_c[:, s, hh * ROW:hh * ROW + ROW], v16[:, s, b, hh, :],
                                   start=True, stop=True)
                        i.then_inc(sg(f"{n}_pv"), 1)
                yield "l3a_ot"
                for s in mine:
                    tile("l3a1_o", s)
                    nc.tensor.transpose(ps(s, 0, P), vtmp[:, s, :], ident[:]).then_inc(sg("l3a_ot"), 1)
                yield "l3a_out"
                for s in mine:
                    tile("l3a_ots", s)
                    mm(ps(s, BANK, D), qt[:, s, :], w_proj3[:], start=True, stop=True).then_inc(sg("l3a_out"), 1)

                yield "l3f_st"
                for s in mine:
                    tile("l3f_diag", s)
                    mm(ps(s, BANK, P), ones[:], vtmp[:, s, :], start=True, stop=True).then_inc(sg("l3f_st"), 1)
                yield from turn_quantised("l3f", 1)
                yield "l3f_hid"
                for s in mine:
                    tile("l3f_qts", s)
                    for c in range(4):
                        i = mm(ps(s, c * P, P), tern[:, 2, c * P:c * P + P], quant_t[:, s, 0:P],
                               start=True, stop=True)
                    i.then_inc(sg("l3f_hid"), 1)
                yield from turn_many("l3f_bent", "l3f_act", lambda s: wide_b[:, s, 0:BANK], 4, 0)
                yield from turn_quantised("l3g", 4)
                yield from down("l3g", 3)

            all_passes(pe, part)


def rotary_table(np):
    half = np.arange(0, ROW, 2, dtype=np.float32)
    freq = np.arange(ROW, dtype=np.float32)[:, None] * (1.0 / 10000.0 ** (half / ROW))[None]
    freq = np.concatenate([freq, freq], -1)
    base = (half + 0.4 * ROW) / (1.4 * ROW)
    scale = base[None] ** ((np.arange(ROW, dtype=np.float32) - ROW // 2) / 32.0)[:, None]
    scale = np.concatenate([scale, scale], -1)
    sign = np.where(np.arange(ROW) < ROW // 2, -1.0, 1.0)[None]
    cos, sin = np.cos(freq), np.sin(freq) * sign
    t = np.stack([np.stack([8 * cos * scale, 8 * sin * scale], 1), np.stack([cos / scale, sin / scale], 1)], 1)
    return np.concatenate([t, t], 0).astype(np.float32)


def laid_out(i):
    import numpy as np

    def rep(a, n=P):
        return np.broadcast_to(a[None], (n,) + a.shape)

    def col(a):
        return a.reshape(-1, 1)

    def heads(w):
        w = w.reshape(2, 8, ROW, D)
        order = [4 * (j % 2) + 2 * k + j // 2 for j in range(4) for k in range(2)]
        return w[:, order].reshape(2, 4, P, D).transpose(2, 0, 1, 3)

    def chunked(a, axis):
        pad = [(0, 0)] * a.ndim
        pad[axis] = (0, FFC * P - FF)
        return np.pad(a, pad)

    w1 = i["L0_ffn_w1"].reshape(2, D, 2, FF)
    b1 = i["L0_ffn_b1"].reshape(2, 2, FF)
    ctx = i["ctx_2048"].reshape(PASSES, G, P, CTX)
    row = np.ascontiguousarray
    wide = lambda w: w.T.reshape(4, P, D).transpose(1, 0, 2).reshape(P, HID)
    a = {
        "x": i["x"].reshape(PASSES, G, P, D),
        "ctx": ctx,
        "ctx_t": ctx.reshape(PASSES, G, P, 2, P).transpose(0, 1, 4, 3, 2),
        "mask_f": i["mask_BxS2_fk1"].reshape(PASSES, G, P),
        "mask_i": i["mask_BxS2_ik0"].reshape(PASSES, G, P),
        "lens_t": i["mask_BxS2_if0"].T,
        "w_src": i["L0_xattn_W_src"].T.reshape(2, P, 2 * D).transpose(1, 0, 2),
        "w_tgt": i["L0_xattn_W_tgt"].T,
        "w_out": i["L0_xattn_W_out"].T.reshape(2, P, D).transpose(1, 0, 2),
        "b_q": col(i["L0_xattn_b_tgt"]), "b_k": col(i["L0_xattn_b_src"][:D]), "b_v": rep(i["L0_xattn_b_src"][D:]),
        "w_qkv": i["L0_ffn_wqkv"].transpose(1, 0, 2), "w_o": heads(i["L0_ffn_wo"]),
        "w_1": chunked(w1, 3).reshape(2, D, 2, FFC, P).transpose(1, 0, 2, 3, 4),
        "w_2": chunked(i["L0_ffn_w2"], 1).reshape(2, FFC, P, D).transpose(2, 0, 1, 3),
        "b_1": chunked(b1, 2).reshape(2, 2, FFC, P).transpose(3, 0, 1, 2),
        "b_2": rep(i["L0_ffn_b2"]), "ln_g": i["L0_ffn_ln_g"].T, "ln_b": i["L0_ffn_ln_b"].T,
        "qk_scale": rep(np.stack([i["L0_ffn_q_scale"], i["L0_ffn_k_scale"]], 1)),
        "rotary": rotary_table(np),
        "w_in": i["L1_xattn_W_in"].T, "g_res": col(i["L1_xattn_g_res"]), "g_init": rep(i["L1_xattn_g_init"][:D]),
        "w_gate": i["L1_ffn_Wg"], "w_a": i["L1_ffn_A"].transpose(1, 0, 2).reshape(D, E * R),
        "w_b": i["L1_ffn_B"].reshape(E * R, D), "logit_b": rep(i["L2_xattn_b"]),
        "tern": np.stack([i["L2_ffn_W1"].T, wide(i["L2_ffn_W2"]), i["L3_ffn_w1"].T, wide(i["L3_ffn_w2"])], 1),
        "b_t1": rep(i["L2_ffn_b1"]),
        "w_qkv3": i["L3_xattn_w_qkv"].T, "w_proj3": i["L3_xattn_w_proj"].T,
        "conv_w": i["L3_ffn_conv_w"].reshape(4, P, 3).transpose(1, 0, 2),
        "conv_b": i["L3_ffn_conv_b"].reshape(4, P).T,
        "gate_in": rep(np.concatenate([i["g_xattn"], i["g_ffn"]])),
        "bias_in": rep(np.stack([i["L0_xattn_b_out"], i["L1_xattn_b_in"], i["L2_ffn_b2"], i["L3_xattn_b_proj"]])),
    }
    return {k: row(v) for k, v in a.items()}


def kernel(**inputs):
    import numpy as np
    import concourse.bacc as bacc
    from concourse.bass_utils import run_bass_kernel_spmd

    nc = bacc.Bacc("TRN2", target_bir_lowering=False, num_devices=1)
    arrays, d = {}, {}
    for name, a in laid_out({k: np.asarray(v) for k, v in inputs.items()}).items():
        arrays[f"in_{name}"] = a
        d[name] = nc.dram_tensor(f"in_{name}", a.shape, mybir.dt.from_np(a.dtype), kind="ExternalInput").ap()
    out = nc.dram_tensor("out", (PASSES, G, P, D), F32, kind="ExternalOutput").ap()
    flamingo_stack(nc, d, out)
    r = run_bass_kernel_spmd(nc, [arrays], core_ids=[0])
    return r.results[0]["out"].reshape(B, ROW, D)
```
